# Optimizing a Trainium2 kernel written in Bass

```python
import numpy as np
import jax
import jax.numpy as jnp

def _softmax(x, axis=-1):
    return jax.nn.softmax(x, axis=axis)

def _gelu(x):
    return jax.nn.gelu(x, approximate=True)

def _silu(x):
    return jax.nn.silu(x)

def _sigmoid(x):
    return jax.nn.sigmoid(x)

def _layernorm(x, axis=-1, eps=1e-05):
    m = jnp.mean(x, axis=axis, keepdims=True)
    v = jnp.var(x, axis=axis, keepdims=True)
    return (x - m) / jnp.sqrt(v + eps)

def _scatter_add(tgt, idx, src, axis=0):
    return tgt.at[idx].add(src)

def _segment_sum(src, seg, n):
    return jax.ops.segment_sum(src, seg, n)
kernel_name = 'mk_cond_seq_d2_seqx_r4_d69f15'

def setup_inputs(seed: int=0):
    np.random.seed(seed)
    _w = jnp.asarray

    def _rec_inputs():
        import jax
        import jax.numpy as jnp
        _rk = jax.random.key(seed)
        x = -0.0003929 + 0.9999 * jax.random.normal(jax.random.fold_in(_rk, 1), (16, 256, 256), jnp.float32)
        _lenS = 256 - jax.random.randint(jax.random.fold_in(_rk, 7), (16,), 0, max(1, 256 // 4) + 1, jnp.int32)
        _lenS2 = 256 - jax.random.randint(jax.random.fold_in(_rk, 8), (16,), 0, max(1, 256 // 4) + 1, jnp.int32)
        cond_1024 = 0.0061147 + 1.02565 * jax.random.normal(jax.random.fold_in(_rk, 11), (16, 256), jnp.float32)
        condB_cfgscale = 0.367289 + 0.966787 * jax.random.normal(jax.random.fold_in(_rk, 12), (16,), jnp.float32)
        return (x, cond_1024, condB_cfgscale)
    x, cond_1024, condB_cfgscale = _rec_inputs()

    def _L0_cond_setup():
        import jax, jax.numpy as jnp
        import numpy as np
        D = 256
        H = 8
        STRIDE = 4
        FFN = 4 * D
        EPS = 1e-06
        NORM_EPS = 1e-12
        RES_ALPHA = 1.0
        CFG_CLAMP = 2.0

        def rmsnorm(x, w):
            return w * x * jax.lax.rsqrt(jnp.mean(x * x, axis=-1, keepdims=True) + EPS)

        def l2norm(x):
            n = jnp.sqrt(jnp.sum(x * x, axis=-1, keepdims=True))
            return x / jnp.maximum(n, NORM_EPS)
        key = jax.random.key(seed)
        ks = jax.random.split(key, 10)
        B, T = (4, 1024)
        s = 0.02
        return {'x': jax.random.normal(ks[0], (B, T, D), jnp.float32), 'style': jax.random.normal(ks[1], (B, 1, D), jnp.float32), 'cfg_scale': jax.random.normal(ks[2], (B,), jnp.float32), 'norm_in_w': jnp.ones((D,), jnp.float32), 'pre_w': jax.random.normal(ks[3], (D, D), jnp.float32) * s, 'harm_w': jax.random.normal(ks[4], (D, 2 * H), jnp.float32) * s, 'harm_b': jnp.zeros((D,), jnp.float32), 'style_w': jax.random.normal(ks[5], (D, D), jnp.float32) * s, 'merge_w': jax.random.normal(ks[6], (D, 2 * D), jnp.float32) * s, 'merge_b': jnp.zeros((D,), jnp.float32), 'ffn_w1': jax.random.normal(ks[7], (FFN, D), jnp.float32) * s, 'ffn_b1': jnp.zeros((FFN,), jnp.float32), 'ffn_w2': jax.random.normal(ks[8], (D, FFN), jnp.float32) * s, 'ffn_b2': jnp.zeros((D,), jnp.float32), 'norm_out_w': jnp.ones((D,), jnp.float32)}
    _L0_cond_all = _L0_cond_setup()
    _L0_cond_in = {k: v for k, v in _L0_cond_all.items() if k in ('norm_in_w', 'pre_w', 'harm_w', 'harm_b', 'style_w', 'merge_w', 'merge_b', 'ffn_w1', 'ffn_b1', 'ffn_w2', 'ffn_b2', 'norm_out_w')}
    del _L0_cond_all

    def _L1_cond_setup():
        import jax, jax.numpy as jnp
        import numpy as np
        B, N, D = (2, 512, 256)
        H, HD = (16, 64)
        E, DD = (8, 1024)
        EPS = 1e-05

        def _ln(x, g, b):
            m = jnp.mean(x, axis=-1, keepdims=True)
            v = jnp.var(x, axis=-1, keepdims=True)
            return (x - m) * jax.lax.rsqrt(v + EPS) * g + b
        key = jax.random.key(seed)
        ks = jax.random.split(key, 16)
        s = 0.02
        return {'x': jax.random.normal(ks[0], (B, N, D), jnp.float32), 't': jax.random.normal(ks[1], (B, 1, D), jnp.float32), 'W_ada': jax.random.normal(ks[2], (D, D), jnp.float32) * s, 'b_ada': jnp.zeros((D,), jnp.float32), 'ln1_g': jnp.ones((D,), jnp.float32), 'ln1_b': jnp.zeros((D,), jnp.float32), 'Wqkv': jax.random.normal(ks[3], (3 * H * HD, D), jnp.float32) * s, 'qn_g': jnp.ones((HD,), jnp.float32), 'qn_b': jnp.zeros((HD,), jnp.float32), 'kn_g': jnp.ones((HD,), jnp.float32), 'kn_b': jnp.zeros((HD,), jnp.float32), 'Wout': jax.random.normal(ks[4], (D, H * HD), jnp.float32) * s, 'mlp_g': jnp.ones((D,), jnp.float32), 'mlp_b': jnp.zeros((D,), jnp.float32), 'Wgate': jax.random.normal(ks[5], (E, D), jnp.float32) * s, 'fc1s': jax.random.normal(ks[6], (E, DD, D), jnp.float32) * s, 'b1s': jnp.zeros((E, DD), jnp.float32), 'fc2s': jax.random.normal(ks[7], (E, D, DD), jnp.float32) * s, 'b2s': jnp.zeros((E, D), jnp.float32)}
    _L1_cond_all = _L1_cond_setup()
    _L1_cond_in = {k: v for k, v in _L1_cond_all.items() if k in ('W_ada', 'b_ada', 'ln1_g', 'ln1_b', 'Wqkv', 'qn_g', 'qn_b', 'kn_g', 'kn_b', 'Wout', 'mlp_g', 'mlp_b', 'Wgate', 'fc1s', 'b1s', 'fc2s', 'b2s')}
    del _L1_cond_all
    return {'x': x, 'cond_1024': cond_1024, 'condB_cfgscale': condB_cfgscale, 'L0_cond_norm_in_w': _L0_cond_in['norm_in_w'], 'L0_cond_pre_w': _L0_cond_in['pre_w'], 'L0_cond_harm_w': _L0_cond_in['harm_w'], 'L0_cond_harm_b': _L0_cond_in['harm_b'], 'L0_cond_style_w': _L0_cond_in['style_w'], 'L0_cond_merge_w': _L0_cond_in['merge_w'], 'L0_cond_merge_b': _L0_cond_in['merge_b'], 'L0_cond_ffn_w1': _L0_cond_in['ffn_w1'], 'L0_cond_ffn_b1': _L0_cond_in['ffn_b1'], 'L0_cond_ffn_w2': _L0_cond_in['ffn_w2'], 'L0_cond_ffn_b2': _L0_cond_in['ffn_b2'], 'L0_cond_norm_out_w': _L0_cond_in['norm_out_w'], 'L1_cond_W_ada': _L1_cond_in['W_ada'], 'L1_cond_b_ada': _L1_cond_in['b_ada'], 'L1_cond_ln1_g': _L1_cond_in['ln1_g'], 'L1_cond_ln1_b': _L1_cond_in['ln1_b'], 'L1_cond_Wqkv': _L1_cond_in['Wqkv'], 'L1_cond_qn_g': _L1_cond_in['qn_g'], 'L1_cond_qn_b': _L1_cond_in['qn_b'], 'L1_cond_kn_g': _L1_cond_in['kn_g'], 'L1_cond_kn_b': _L1_cond_in['kn_b'], 'L1_cond_Wout': _L1_cond_in['Wout'], 'L1_cond_mlp_g': _L1_cond_in['mlp_g'], 'L1_cond_mlp_b': _L1_cond_in['mlp_b'], 'L1_cond_Wgate': _L1_cond_in['Wgate'], 'L1_cond_fc1s': _L1_cond_in['fc1s'], 'L1_cond_b1s': _L1_cond_in['b1s'], 'L1_cond_fc2s': _L1_cond_in['fc2s'], 'L1_cond_b2s': _L1_cond_in['b2s']}

def reference(x, cond_1024, condB_cfgscale, L0_cond_norm_in_w, L0_cond_pre_w, L0_cond_harm_w, L0_cond_harm_b, L0_cond_style_w, L0_cond_merge_w, L0_cond_merge_b, L0_cond_ffn_w1, L0_cond_ffn_b1, L0_cond_ffn_w2, L0_cond_ffn_b2, L0_cond_norm_out_w, L1_cond_W_ada, L1_cond_b_ada, L1_cond_ln1_g, L1_cond_ln1_b, L1_cond_Wqkv, L1_cond_qn_g, L1_cond_qn_b, L1_cond_kn_g, L1_cond_kn_b, L1_cond_Wout, L1_cond_mlp_g, L1_cond_mlp_b, L1_cond_Wgate, L1_cond_fc1s, L1_cond_b1s, L1_cond_fc2s, L1_cond_b2s):
    import jax
    import jax.numpy as jnp

    def _L0_cond_ref(x, style, cfg_scale, norm_in_w, pre_w, harm_w, harm_b, style_w, merge_w, merge_b, ffn_w1, ffn_b1, ffn_w2, ffn_b2, norm_out_w):
        import jax, jax.numpy as jnp
        import numpy as np
        D = 256
        H = 8
        STRIDE = 4
        FFN = 4 * D
        EPS = 1e-06
        NORM_EPS = 1e-12
        RES_ALPHA = 1.0
        CFG_CLAMP = 2.0

        def rmsnorm(x, w):
            return w * x * jax.lax.rsqrt(jnp.mean(x * x, axis=-1, keepdims=True) + EPS)

        def l2norm(x):
            n = jnp.sqrt(jnp.sum(x * x, axis=-1, keepdims=True))
            return x / jnp.maximum(n, NORM_EPS)
        B, T, _ = x.shape
        z = rmsnorm(x, norm_in_w) @ pre_w.T
        t = jnp.arange(T)
        folded = jnp.zeros_like(z)
        for w in range(STRIDE):
            folded = folded + jnp.take(z, jnp.minimum(t + w, T - 1), axis=1)
        folded = folded / STRIDE
        mask = (t < T - (STRIDE - 1)).astype(x.dtype)[None, :, None]
        posf = (t / max(1, T - 1)).astype(x.dtype)
        kf = jnp.arange(1, H + 1, dtype=x.dtype)
        ang = 2.0 * jnp.pi * posf[:, None] * kf[None, :]
        Hst = jnp.stack([jnp.sin(ang), jnp.cos(ang)], axis=-1).reshape(T, 2 * H)
        gate = jax.nn.sigmoid(Hst @ harm_w.T + harm_b)[None]
        gfold = folded * gate
        styleT = jnp.broadcast_to(style, (B, T, D)) if style.shape[1] == 1 else style
        target = styleT @ style_w.T
        cfg = jnp.clip(cfg_scale.reshape(B, 1, 1), -CFG_CLAMP, CFG_CLAMP).astype(x.dtype)
        cos = jnp.sum(l2norm(gfold) * l2norm(target), axis=-1, keepdims=True)
        scale = cfg * (1.0 + cos) * 0.5
        cfg_blend = gfold + scale * (target - gfold)
        merged = jnp.concatenate([x, cfg_blend], axis=-1)
        y = merged @ merge_w.T + merge_b
        h = rmsnorm(y, norm_out_w)
        h = jax.nn.gelu(h @ ffn_w1.T + ffn_b1, approximate=False)
        y = h @ ffn_w2.T + ffn_b2 + RES_ALPHA * x
        return y

    def _L1_cond_ref(x, t, W_ada, b_ada, ln1_g, ln1_b, Wqkv, qn_g, qn_b, kn_g, kn_b, Wout, mlp_g, mlp_b, Wgate, fc1s, b1s, fc2s, b2s):
        import jax, jax.numpy as jnp
        import numpy as np
        B, N, D = (2, 512, 256)
        H, HD = (16, 64)
        E, DD = (8, 1024)
        EPS = 1e-05

        def _ln(x, g, b):
            m = jnp.mean(x, axis=-1, keepdims=True)
            v = jnp.var(x, axis=-1, keepdims=True)
            return (x - m) * jax.lax.rsqrt(v + EPS) * g + b
        b, n, d = x.shape
        shift = jax.nn.silu(t) @ W_ada.T + b_ada
        h = _ln(x, ln1_g, ln1_b) + shift
        qkv = (h @ Wqkv.T).reshape(b, n, 3, H, HD)
        q = _ln(qkv[:, :, 0].transpose(0, 2, 1, 3), qn_g, qn_b)
        k = _ln(qkv[:, :, 1].transpose(0, 2, 1, 3), kn_g, kn_b)
        v = qkv[:, :, 2].transpose(0, 2, 1, 3)
        scores = jnp.einsum('bhnd,bhmd->bhnm', q, k) / jnp.sqrt(jnp.float32(HD))
        attn = jax.nn.softmax(scores, axis=-1)
        o = jnp.einsum('bhnm,bhmd->bhnd', attn, v)
        o = o.transpose(0, 2, 1, 3).reshape(b, n, H * HD)
        x = x + o @ Wout.T
        tok = x.reshape(-1, d)
        bs = tok.shape[0]
        gate = jax.nn.softmax(tok @ Wgate.T, axis=-1)
        k_cap = bs // E
        vals, idx = jax.lax.top_k(gate.T, k_cap)
        idx_flat = idx.T.reshape(-1)
        w = vals.T
        g = _ln(tok[idx_flat], mlp_g, mlp_b).reshape(k_cap, E, d)
        y = jnp.einsum('ked,ehd->keh', g, fc1s) + b1s
        y = jax.nn.gelu(y, approximate=True)
        y = jnp.einsum('keh,edh->ked', y, fc2s) + b2s
        y = y * w[..., None]
        tok = tok.at[idx_flat].add(y.reshape(-1, d))
        return tok.reshape(x.shape)
    x = _L0_cond_ref(x, cond_1024[:, None, :], condB_cfgscale, L0_cond_norm_in_w, L0_cond_pre_w, L0_cond_harm_w, L0_cond_harm_b, L0_cond_style_w, L0_cond_merge_w, L0_cond_merge_b, L0_cond_ffn_w1, L0_cond_ffn_b1, L0_cond_ffn_w2, L0_cond_ffn_b2, L0_cond_norm_out_w)
    x = _L1_cond_ref(x, cond_1024[:, None, :], L1_cond_W_ada, L1_cond_b_ada, L1_cond_ln1_g, L1_cond_ln1_b, L1_cond_Wqkv, L1_cond_qn_g, L1_cond_qn_b, L1_cond_kn_g, L1_cond_kn_b, L1_cond_Wout, L1_cond_mlp_g, L1_cond_mlp_b, L1_cond_Wgate, L1_cond_fc1s, L1_cond_b1s, L1_cond_fc2s, L1_cond_b2s)
    return x

_drawn_inputs = setup_inputs


def setup_inputs(seed=0):
    import zlib

    import numpy as np

    out = dict(_drawn_inputs(seed))
    spreads = {'L0_cond_norm_in_w': (1.0, 0.6),
     'L0_cond_harm_b': (0.0, 2.0),
     'L0_cond_merge_b': (0.0, 0.1),
     'L0_cond_ffn_b1': (0.0, 0.1),
     'L0_cond_ffn_b2': (0.0, 0.1),
     'L0_cond_norm_out_w': (1.0, 0.6),
     'L1_cond_b_ada': (0.0, 0.341),
     'L1_cond_ln1_g': (1.0, 0.6),
     'L1_cond_ln1_b': (0.0, 0.429),
     'L1_cond_qn_g': (1.0, 0.6),
     'L1_cond_qn_b': (0.0, 0.8),
     'L1_cond_kn_g': (1.0, 0.6),
     'L1_cond_kn_b': (0.0, 2.0),
     'L1_cond_mlp_g': (1.0, 0.6),
     'L1_cond_mlp_b': (0.0, 2.0),
     'L1_cond_b1s': (0.0, 0.8),
     'L1_cond_b2s': (0.0, 0.429)}
    factors = {'condB_cfgscale': 3.439,
     'L0_cond_pre_w': 6.097,
     'L0_cond_harm_w': 25.663,
     'L0_cond_style_w': 3.665}
    for name, (base, spread) in spreads.items():
        noise = np.random.default_rng([zlib.crc32(name.encode()), seed]).standard_normal(out[name].shape)
        drawn = base * np.exp(spread * noise) if base else spread * noise
        out[name] = jnp.asarray(drawn.astype(out[name].dtype))
    for name, factor in factors.items():
        out[name] = (out[name] * factor).astype(out[name].dtype)
    return out
```

```python
from contextlib import ExitStack

import numpy as np

import concourse.bass as bass
from concourse import mybir

F32 = mybir.dt.float32
F32R = mybir.dt.float32r
I32 = mybir.dt.int32
U32 = mybir.dt.uint32
ALU = mybir.AluOpType
ACT = mybir.ActivationFunctionType
AX = mybir.AxisListType.X

P = 128
NB, T, D = 16, 256, 256
TT, KT = T // P, D // P
TOKENS = NB * T
TILES = TOKENS // P
F1 = 1024
G1 = F1 // (2 * P)
H, HD = 16, 64
HW = H * HD
E, DD = 8, 1024
CAP = TOKENS // E
CC = CAP // P
G2 = DD // P
RMS_EPS, LN_EPS, NORM_EPS = 1e-6, 1e-5, 1e-12
MAGIC = 0x5F3759DF


def live(b):
    return not isinstance(b, int) or 0 <= b < NB


def wait(eng, sem, per, b, n):
    if n <= 0:
        b, n = b - 1, n + per
    if live(b):
        eng.wait_ge(sem, b * per + n)


def head_at(t, i, lag, odd):
    return (t, i - lag, odd) if i >= lag else (t - 1, i - lag + H, 1 - odd)


def chunk_at(t, i):
    if i < 0:
        t, i = t - 1, i + SLOTS
    if i not in CHUNK_SLOTS:
        return t, None
    j = CHUNK_SLOTS.index(i)
    return (t + 2 if j < AHEAD else t + 1), j


class Links:

    def __init__(self, eng, sem):
        self.eng, self.sem, self.base, self.n = eng, sem, 0, 0

    def __call__(self, ins):
        ins.then_inc(self.sem, 1)
        self.n += 1
        self.eng.wait_ge(self.sem, self.base + self.n)

    def settle(self):
        self.eng.wait_ge(self.sem, self.base + self.n)

    def note(self, ins):
        ins.then_inc(self.sem, 1)
        self.n += 1

    def enter(self, i, per):
        self.before = self.base + self.n
        self.base, self.n, self.per = self.before + i * per, 0, per

    def leave(self, count):
        assert self.n == self.per, f"the loop's body has {self.n} links"
        self.base, self.n = self.before + count * self.per, 0


RSQRT_OPS, MOMENTS_OPS = 11, 7


def rsqrt_op(nc, k, v, y, t):
    vec = nc.vector
    if k == 0:
        return vec.tensor_scalar(t.bitcast(I32), v.bitcast(I32), 1, None, ALU.logical_shift_right)
    if k == 1:
        return vec.tensor_scalar(y.bitcast(I32), t.bitcast(I32), -1.0, float(MAGIC), ALU.mult, ALU.add)
    if k % 3 == 2:
        return vec.tensor_tensor(t, y, y, ALU.mult)
    if k % 3 == 0:
        return vec.scalar_tensor_tensor(t, t, -0.5, v, ALU.mult, ALU.mult)
    return vec.scalar_tensor_tensor(y, t, 1.5, y, ALU.add, ALU.mult)


def moments_op(nc, k, stats, mean, var, d):
    vec = nc.vector
    if k == 0:
        return vec.tensor_tensor(d, stats[:, :, 1], stats[:, :, 4], ALU.subtract)
    if k == 1:
        return vec.tensor_tensor(mean, stats[:, :, 1], stats[:, :, 4], ALU.add)
    if k == 2:
        return vec.tensor_tensor(var, stats[:, :, 2], stats[:, :, 5], ALU.add)
    if k == 3:
        return vec.tensor_tensor(d, d, d, ALU.mult)
    if k == 4:
        return vec.tensor_scalar(mean, mean, 0.5, None, ALU.mult)
    if k == 5:
        return vec.tensor_scalar(var, var, 1.0 / D, LN_EPS, ALU.mult, ALU.add)
    return vec.scalar_tensor_tensor(var, d, 0.25, var, ALU.mult, ALU.add)


def rsqrt(nc, link, v, y, t):
    for k in range(RSQRT_OPS):
        link(rsqrt_op(nc, k, v, y, t))


def moments(nc, link, stats, mean, var, d):
    for k in range(MOMENTS_OPS):
        ins = moments_op(nc, k, stats, mean, var, d)
        if k in (2, 5, 6):
            link(ins)


def product(nc, out, lhs, rhs, ks):
    n = 0
    for k in ks:
        (ah, al), (bh, bl) = lhs(k), rhs(k)
        for a, b in ((ah, bh), (ah, bl), (al, bh)):
            last = nc.tensor.matmul(out, a, b, start=(n == 0), stop=(n == 3 * len(ks) - 1))
            n += 1
    return last


def build(nc, a, out):
    top = ExitStack()
    with top:
        def sbuf(stack, name, shape, dt=F32):
            return stack.enter_context(nc.sbuf_tensor(name, shape, dt))

        def sems(stack, names):
            return [stack.enter_context(nc.semaphore(n)) for n in names.split()]

        banks = [top.enter_context(nc.psum_tensor(f"bank{i}", [P, 512], F32)) for i in range(8)]
        ident = sbuf(top, "ident", [P, P])
        hbias = sbuf(top, "hbias", [P, KT, NB])
        cols = sbuf(top, "cols", [P, 30])
        x1_rows = nc.dram_tensor("x1_rows", [TOKENS, D], F32).ap()
        target_rows = nc.dram_tensor("target_rows", [NB, D + 2], F32).ap()
        x2_rows = nc.dram_tensor("x2_rows", [TOKENS, D], F32).ap()
        logit = sbuf(top, "logit", [P, TILES, E])

        first_block(nc, a, banks, ident, x1_rows, hbias, cols, target_rows, sbuf, sems)
        attention(nc, a, banks, ident, x1_rows, hbias, cols, x2_rows, logit, out, sbuf, sems)
        experts(nc, a, banks, ident, cols, x2_rows, logit, out, sbuf, sems)


NORM_IN, NORM_OUT, LN1_G, LN1_B, B_ADA, MLP_G, MLP_B = (0, 2, 4, 6, 8, 10, 12)
QN_G, QN_B, KN_G, KN_B = (14, 15, 16, 17)
FFN_B1 = 18


def first_block(nc, a, banks, ident, x1_rows, hbias, cols, target_rows, sbuf, sems):
    s = ExitStack()
    with s:
        pre_h, pre_l = (sbuf(s, f"pre_{p}", [P, KT, D], F32R) for p in "hl")
        mrg_h, mrg_l = (sbuf(s, f"mrg_{p}", [P, 2 * KT, D], F32R) for p in "hl")
        w1_h, w1_l = (sbuf(s, f"w1_{p}", [P, KT, F1], F32R) for p in "hl")
        w2_h, w2_l = (sbuf(s, f"w2_{p}", [P, F1 // P, D], F32R) for p in "hl")
        gate = sbuf(s, "gate", [P, TT, D])
        merge_b, ffn_b2 = sbuf(s, "merge_b", [P, D]), sbuf(s, "ffn_b2", [P, D])

        with ExitStack() as u:
            raw = sbuf(u, "raw", [P, 5632])
            cond_t, silu_t = sbuf(u, "cond_t", [P, KT, NB]), sbuf(u, "silu_t", [P, KT, NB])
            style_w, ada_w = sbuf(u, "style_w", [P, KT, D]), sbuf(u, "ada_w", [P, KT, D])
            harm, harm_w = sbuf(u, "harm", [16, T]), sbuf(u, "harm_w", [16, D])
            harm_b = sbuf(u, "harm_b", [P, D])
            trow = sbuf(u, "trow", [NB, D + 2])
            tsq, tss, tmp = sbuf(u, "tsq", [NB, D]), sbuf(u, "tss", [NB, 1]), sbuf(u, "tmp", [NB, 1])
            cfg = sbuf(u, "cfg", [NB, 1])
            (weights_in, consts_in, vectors_in, hi_done, lo_done, silu_done, style_done, target_done,
             ada_done, hbias_done, harm_done, gate_sum, gate_done, target_sq, links, row_done,
             row_out) = sems(u, "weights_in consts_in vectors_in hi_done lo_done silu_done "
                             "style_done target_done ada_done hbias_done harm_done gate_sum "
                             "gate_done target_sq setup_links row_done row_out")
            pieces = [(pre_h, pre_l, 0, KT * D, a["pre_w"], KT), (mrg_h, mrg_l, 512, 2 * KT * D, a["merge_w"], 2 * KT),
                      (w1_h, w1_l, 1536, KT * F1, a["ffn_w1"], KT), (w2_h, w2_l, 3584, F1 // P * D, a["ffn_w2"], F1 // P)]
            with nc.Block() as block:
                @block.sync
                def _(sp):
                    for t, src in ((ident[:, :], a["ident"]), (harm[:, :], a["harm"]), (harm_w[:, :], a["harm_w"]),
                                   (harm_b[:, :], a["harm_b"].unsqueeze(0).to_broadcast([P, D])),
                                   (cond_t[:, :, :], a["cond"].rearrange("(k p) b -> p k b", p=P)),
                                   (style_w[:, :, :], a["style_w"].rearrange("(k p) n -> p k n", p=P)),
                                   (ada_w[:, :, :], a["W_ada"].rearrange("(k p) n -> p k n", p=P)),
                                   (cfg[:, :], a["cfg"])):
                        sp.dma_start(t, src).then_inc(consts_in, 16)
                    for _, _, at, n, src, k in pieces:
                        sp.dma_start(raw[:, at:at + n].rearrange("p (k n) -> p k n", k=k),
                                     src.rearrange("(k p) n -> p k n", p=P)).then_inc(weights_in, 16)
                    sp.wait_ge(row_done, 1)
                    sp.dma_start(target_rows, trow[:, :]).then_inc(row_out, 16)
                    sp.wait_ge(row_out, 16)

                @block.scalar
                def _(act):
                    act.dma_start(cols[:, :], a["cols"]).then_inc(vectors_in, 16)
                    act.dma_start(merge_b[:, :], a["merge_b"].unsqueeze(0).to_broadcast([P, D])).then_inc(vectors_in, 16)
                    act.dma_start(ffn_b2[:, :], a["ffn_b2"].unsqueeze(0).to_broadcast([P, D])).then_inc(vectors_in, 16)
                    act.wait_ge(consts_in, 16 * 8)
                    nc.scalar.activation(silu_t[:, :, :], cond_t[:, :, :], ACT.Silu).then_inc(silu_done, 1)
                    act.wait_ge(style_done, 1)
                    nc.scalar.activation(tsq[:, :], banks[0][0:NB, 0:D], ACT.Square, accum_out=tss[:, :]).then_inc(target_sq, 1)
                    act.wait_ge(weights_in, 64)
                    for hi, _, at, n, _, _ in pieces:
                        nc.scalar.activation(hi[:, :, :].rearrange("p k n -> p (k n)"), raw[:, at:at + n], ACT.Copy).then_inc(hi_done, 1)
                    act.wait_ge(gate_sum, 1)
                    nc.scalar.activation(gate[:, :, :], gate[:, :, :], ACT.Sigmoid).then_inc(gate_done, 1)
                    act.wait_ge(vectors_in, 48)

                @block.gpsimd
                def _(pool):
                    for i, (hi, lo, at, n, _, _) in enumerate(pieces):
                        pool.wait_ge(hi_done, i + 1)
                        nc.gpsimd.tensor_tensor(lo[:, :, :].rearrange("p k n -> p (k n)"), raw[:, at:at + n],
                                                hi[:, :, :].rearrange("p k n -> p (k n)").bitcast(F32),
                                                ALU.subtract).then_inc(lo_done, 1)

                @block.tensor
                def _(pe):
                    pe.wait_ge(consts_in, 16 * 8)
                    for k in range(KT):
                        last = nc.tensor.matmul(banks[0][0:NB, 0:D], cond_t[:, k, :], style_w[:, k, :],
                                                start=(k == 0), stop=(k == KT - 1))
                    last.then_inc(style_done, 1)
                    for t in range(TT):
                        last = nc.tensor.matmul(banks[1][:, t * D:(t + 1) * D], harm[:, t * P:(t + 1) * P], harm_w[:, :],
                                                start=True, stop=True)
                    last.then_inc(harm_done, 1)
                    pe.wait_ge(silu_done, 1)
                    for m in range(KT):
                        for k in range(KT):
                            last = nc.tensor.matmul(banks[2][:, m * NB:(m + 1) * NB], ada_w[:, k, m * P:(m + 1) * P],
                                                    silu_t[:, k, :], start=(k == 0), stop=(k == KT - 1))
                    last.then_inc(ada_done, 1)

                @block.vector
                def _(dve):
                    link = Links(dve, links)
                    dve.wait_ge(consts_in, 16 * 8)
                    dve.wait_ge(vectors_in, 48)
                    link(nc.vector.tensor_scalar(cfg[:, :], cfg[:, :], 2.0, -2.0, ALU.min, ALU.max))
                    link(nc.vector.tensor_scalar(trow[:, D + 1:D + 2], cfg[:, :], 0.5, None, ALU.mult))
                    dve.wait_ge(target_sq, 1)
                    link(nc.vector.tensor_copy(trow[:, 0:D], banks[0][0:NB, 0:D]))
                    link(nc.vector.tensor_scalar(tss[:, :], tss[:, :], NORM_EPS ** 2, None, ALU.max))
                    rsqrt(nc, link, tss[:, :], trow[:, D:D + 1], tmp[:, :])
                    nc.vector.tensor_copy(cfg[:, :], cfg[:, :]).then_inc(row_done, 1)
                    dve.wait_ge(ada_done, 1)
                    for m in range(KT):
                        link(nc.vector.tensor_scalar(hbias[:, m, :], banks[2][:, m * NB:(m + 1) * NB],
                                                     cols[:, LN1_B + m:LN1_B + m + 1], cols[:, B_ADA + m:B_ADA + m + 1],
                                                     ALU.add, ALU.add))
                    dve.wait_ge(harm_done, 1)
                    for t in range(TT):
                        last = nc.vector.tensor_tensor(gate[:, t, :], banks[1][:, t * D:(t + 1) * D], harm_b[:, :], ALU.add)
                    last.then_inc(gate_sum, 1)
                    dve.wait_ge(gate_done, 1)
                    link(nc.vector.tensor_scalar(gate[:, :, :], gate[:, :, :], 0.25, None, ALU.mult))

        x_again, x_b2, x1 = (sbuf(s, n, [P, TT, D]) for n in ("x_again", "x_b2", "x1"))
        x_t = sbuf(s, "x_t", [P, TT, D])
        xT = sbuf(s, "xT", [P, KT, T])
        xT_h, xT_l = (sbuf(s, f"xT_{p}", [P, KT, T], F32R) for p in "hl")
        trow_b = sbuf(s, "trow_b", [P, D + 2])
        junk_act, junk = sbuf(s, "junk_act", [P, 3 * TT, D]), sbuf(s, "junk", [P, D])
        sums, root, root_t = (sbuf(s, n, [P, 3 * TT]) for n in ("sums", "root", "root_t"))
        OF_X, OF_Y, OF_G = 0, TT, 2 * TT
        dots, mix, keep = (sbuf(s, n, [P, TT]) for n in ("dots", "mix", "keep"))
        xn = sbuf(s, "xn", [P, TT, D])
        xnT = sbuf(s, "xnT", [P, KT, T + 3])
        pair = sbuf(s, "pair", [P, KT, T + 2])
        fold = sbuf(s, "fold", [P, KT, T])
        fold_h, fold_l = (sbuf(s, f"fold_{p}", [P, KT, T], F32R) for p in "hl")
        gf = sbuf(s, "gf", [P, TT, D])
        gfs = sbuf(s, "gfs", [P, TT, D])
        blend = sbuf(s, "blend", [P, TT, D])
        bl_h, bl_l = (sbuf(s, f"bl_{p}", [P, KT, T], F32R) for p in "hl")
        y = sbuf(s, "y", [P, TT, D])
        hn = sbuf(s, "hn", [P, TT, D])
        hT = sbuf(s, "hT", [P, KT, T])
        h_h, h_l = (sbuf(s, f"h_{p}", [P, KT, T], F32R) for p in "hl")
        hid = sbuf(s, "hid", [P, F1 // P, T])
        hid_h, hid_l = (sbuf(s, f"hid_{p}", [P, F1 // P, T], F32R) for p in "hl")
        xn_bank, pre_bank, mrg_bank, out_bank, hn_bank, bl_bank = banks[0], banks[1], banks[2], banks[3], banks[6], banks[7]
        ffn_bank = banks[4:6]

        (sums_set, x_in, xT_in, row_in, x_squared, x_scaled, x_kept, xn_T, xnT_out, padded, paired, folded, fold_split,
         pre_done, gf_done, gf_squared, dotted, blended, bl_T, bl_hi, bl_lo, xT_hi, xT_lo, mrg_done, y_done, y_squared,
         hn_done, h_T, hT_out, h_split, ffn1_done, gelu_done, hid_hi, hid_lo, ffn2_done, x1_done, x_again_in, x1_out,
         links) = sems(s, "sums_set x_in xT_in row_in x_squared x_scaled x_kept xn_T xnT_out padded paired folded fold_split "
                       "pre_done gf_done gf_squared dotted blended bl_T bl_hi bl_lo xT_hi xT_lo mrg_done y_done y_squared "
                       "hn_done h_T hT_out h_split ffn1_done gelu_done hid_hi hid_lo ffn2_done x1_done x_again_in x1_out "
                       "first_links")
        FIRST, LOOP, LAST = -3, 2, NB
        LOOPS = NB - 3 - LOOP

        def steps(eng, step, link=None, per=0):
            for t in range(FIRST, LOOP):
                step(t)
            with eng.Fori(0, LOOPS) as i:
                if link:
                    link.enter(i, per)
                step(i + LOOP)
                if link:
                    link.leave(LOOPS)
            for t in range(NB - 3, LAST + 1):
                step(t)

        with nc.Block() as block:
            @block.sync
            def _(sp):
                def step(t):
                    b = t + 3
                    if live(b):
                        wait(sp, x_scaled, 1, b - 1, 1)
                        sp.dma_start(x_t[:, :, :], a["x"][bass.ds(b * T, T), :].rearrange("(t p) d -> p t d", p=P)).then_inc(x_in, 16)
                    b = t + 2
                    if live(b):
                        wait(sp, blended, 1, b - 1, 1)
                        sp.dma_start(trow_b[:, :], target_rows[bass.ds(b, 1), :].to_broadcast([P, D + 2])).then_inc(row_in, 16)
                        wait(sp, xT_lo, 1, b - 1, 1)
                        sp.dma_start(xT[:, :, :], a["xT"][bass.ds(b * D, D), :].rearrange("(k p) t -> p k t", p=P)).then_inc(xT_in, 16)
                    b = t - 1
                    if live(b):
                        wait(sp, x1_done, 1, b, 1)
                        sp.dma_start(x1_rows[bass.ds(b * T, T), :].rearrange("(t p) d -> p t d", p=P), x1[:, :, :]).then_inc(x1_out, 16)
                    b = t
                    if live(b):
                        wait(sp, x_kept, 1, b - 1, 1)
                        sp.dma_start(x_again[:, :, :], a["x"][bass.ds(b * T, T), :].rearrange("(t p) d -> p t d", p=P)).then_inc(x_again_in, 16)
                steps(sp, step)
                sp.wait_ge(x1_out, 16 * NB)

            @block.tensor
            def _(pe):
                def transposes(bank, src):
                    for k in range(KT):
                        for t in range(TT):
                            last = nc.tensor.transpose(bank[:, k * T + t * P:k * T + (t + 1) * P], src[:, t, k * P:(k + 1) * P], ident[:, :])
                    return last

                def pre(b):
                    wait(pe, fold_split, 1, b, 1)
                    wait(pe, gf_done, 1, b - 1, 1)
                    for t in range(TT):
                        last = product(nc, pre_bank[:, t * D:(t + 1) * D],
                                       lambda k: (fold_h[:, k, t * P:(t + 1) * P], fold_l[:, k, t * P:(t + 1) * P]),
                                       lambda k: (pre_h[:, k, :], pre_l[:, k, :]), range(KT))
                    last.then_inc(pre_done, 1)

                def ffn1(b, g):
                    wait(pe, h_split, 1, b, 1)
                    wait(pe, gelu_done, G1, b, g - 1)
                    for m in (2 * g, 2 * g + 1):
                        last = product(nc, ffn_bank[g % 2][:, m % 2 * T:(m % 2 + 1) * T],
                                       lambda k: (w1_h[:, k, m * P:(m + 1) * P], w1_l[:, k, m * P:(m + 1) * P]),
                                       lambda k: (h_h[:, k, :], h_l[:, k, :]), range(KT))
                    last.then_inc(ffn1_done, 1)

                def ffn2(b, t):
                    def hidden(k):
                        if t == 0 and k % 2 == 0:
                            wait(pe, hid_lo, G1, b, k // 2 + 1)
                        return hid_h[:, k, t * P:(t + 1) * P], hid_l[:, k, t * P:(t + 1) * P]
                    wait(pe, x1_done, 1, b - 1, 1)
                    product(nc, out_bank[:, t * D:(t + 1) * D], hidden,
                            lambda k: (w2_h[:, k, :], w2_l[:, k, :]), range(F1 // P)).then_inc(ffn2_done, 1)

                def merge(b):
                    wait(pe, bl_lo, 1, b, 1)
                    wait(pe, xT_lo, 1, b, 1)
                    wait(pe, y_done, 1, b - 1, 1)
                    for t in range(TT):
                        def parts(k):
                            hi, lo = (xT_h, xT_l) if k < KT else (bl_h, bl_l)
                            return hi[:, k % KT, t * P:(t + 1) * P], lo[:, k % KT, t * P:(t + 1) * P]
                        last = product(nc, mrg_bank[:, t * D:(t + 1) * D], parts,
                                       lambda k: (mrg_h[:, k, :], mrg_l[:, k, :]), range(2 * KT))
                    last.then_inc(mrg_done, 1)

                def step(t):
                    old, now, nxt, far = t - 1, t, t + 1, t + 2
                    if live(now):
                        wait(pe, hn_done, 1, now, 1)
                        wait(pe, hT_out, 1, now - 1, 1)
                        transposes(hn_bank, hn).then_inc(h_T, 1)
                    if live(far):
                        wait(pe, x_scaled, 1, far, 1)
                        wait(pe, xnT_out, 1, far - 1, 1)
                        transposes(xn_bank, xn).then_inc(xn_T, 1)
                    if live(old):
                        ffn2(old, 0)
                        ffn2(old, 1)
                    if live(nxt):
                        wait(pe, blended, 1, nxt, 1)
                        wait(pe, bl_lo, 1, nxt - 1, 1)
                        transposes(bl_bank, blend).then_inc(bl_T, 1)
                    if live(far):
                        pre(far)
                    if live(now):
                        ffn1(now, 0)
                    if live(nxt):
                        merge(nxt)
                    if live(now):
                        for g in range(1, G1):
                            ffn1(now, g)
                steps(pe, step)

            @block.scalar
            def _(act):
                def gelu(b, g):
                    wait(act, ffn1_done, G1, b, g + 1)
                    wait(act, ffn2_done, TT, b - 1, TT)
                    wait(act, hid_lo, G1, b - 1, G1)
                    for m in (2 * g, 2 * g + 1):
                        last = nc.scalar.activation(hid[:, m, :], ffn_bank[g % 2][:, m % 2 * T:(m % 2 + 1) * T], ACT.Gelu,
                                                    bias=cols[:, FFN_B1 + m:FFN_B1 + m + 1])
                    last.then_inc(gelu_done, 1)
                    wait(act, gelu_done, G1, b, g + 1)
                    nc.scalar.activation(hid_h[:, 2 * g:2 * g + 2, :], hid[:, 2 * g:2 * g + 2, :], ACT.Copy).then_inc(hid_hi, 1)

                def squares(src, at):
                    for i in range(TT):
                        last = nc.scalar.activation(junk_act[:, at + i, :], src[:, i, :], ACT.Square, accum_out=sums[:, at + i:at + i + 1])
                    return last

                act.wait_ge(sums_set, 1)

                def step(t):
                    now, nxt, far, new = t, t + 1, t + 2, t + 3
                    if live(now):
                        wait(act, h_T, 1, now, 1)
                        wait(act, h_split, 1, now - 1, 1)
                        for k in range(KT):
                            last = nc.scalar.activation(hT[:, k, :], hn_bank[:, k * T:(k + 1) * T], ACT.Copy,
                                                        scale=cols[:, NORM_OUT + k:NORM_OUT + k + 1])
                        last.then_inc(hT_out, 1)
                    if live(far):
                        wait(act, xn_T, 1, far, 1)
                        wait(act, folded, 1, far - 1, 1)
                        for k in range(KT):
                            last = nc.scalar.activation(xnT[:, k, 0:T], xn_bank[:, k * T:(k + 1) * T], ACT.Copy,
                                                        scale=cols[:, NORM_IN + k:NORM_IN + k + 1])
                        last.then_inc(xnT_out, 1)
                    if live(nxt):
                        wait(act, xT_in, 16, nxt, 16)
                        wait(act, mrg_done, 1, nxt - 1, 1)
                        nc.scalar.activation(xT_h[:, :, :], xT[:, :, :], ACT.Copy).then_inc(xT_hi, 1)
                    if live(new):
                        wait(act, x_in, 16, new, 16)
                        wait(act, x_scaled, 1, new - 1, 1)
                        squares(x_t, OF_X).then_inc(x_squared, 1)
                    if live(nxt):
                        wait(act, bl_T, 1, nxt, 1)
                        nc.scalar.activation(bl_h[:, :, :].rearrange("p k t -> p (k t)"), bl_bank[:, :], ACT.Copy).then_inc(bl_hi, 1)
                    if live(far):
                        wait(act, gf_done, 1, far, 1)
                        squares(gf, OF_G).then_inc(gf_squared, 1)
                    if live(now):
                        gelu(now, 0)
                    if live(nxt):
                        wait(act, y_done, 1, nxt, 1)
                        squares(y, OF_Y).then_inc(y_squared, 1)
                    if live(now):
                        for g in range(1, G1):
                            gelu(now, g)
                steps(act, step)

            @block.gpsimd
            def _(pool):
                def hidden_low(b, g):
                    wait(pool, hid_hi, G1, b, g + 1)
                    nc.gpsimd.tensor_tensor(hid_l[:, 2 * g:2 * g + 2, :], hid[:, 2 * g:2 * g + 2, :],
                                            hid_h[:, 2 * g:2 * g + 2, :].bitcast(F32), ALU.subtract).then_inc(hid_lo, 1)

                nc.gpsimd.memset(sums[:, :], 1.0).then_inc(sums_set, 1)

                def step(t):
                    old, now, nxt, far = t - 1, t, t + 1, t + 2
                    if live(old):
                        hidden_low(old, G1 - 1)
                    if live(far):
                        wait(pool, padded, 1, far, 1)
                        nc.gpsimd.tensor_tensor(pair[:, :, :], xnT[:, :, 0:T + 2], xnT[:, :, 1:T + 3], ALU.add).then_inc(paired, 1)
                        wait(pool, paired, 1, far, 1)
                        wait(pool, fold_split, 1, far - 1, 1)
                        nc.gpsimd.tensor_tensor(fold[:, :, :], pair[:, :, 0:T], pair[:, :, 2:T + 2], ALU.add).then_inc(folded, 1)
                    if live(old):
                        wait(pool, x_again_in, 16, old, 16)
                        wait(pool, x1_done, 1, old - 1, 1)
                        nc.gpsimd.tensor_tensor(x_b2[:, :, :], x_again[:, :, :], ffn_b2[:, :].unsqueeze(1).to_broadcast([P, TT, D]), ALU.add).then_inc(x_kept, 1)
                    if live(nxt):
                        wait(pool, xT_hi, 1, nxt, 1)
                        nc.gpsimd.tensor_tensor(xT_l[:, :, :], xT[:, :, :], xT_h[:, :, :].bitcast(F32), ALU.subtract).then_inc(xT_lo, 1)
                    if live(now):
                        for g in range(G1 - 1):
                            hidden_low(now, g)
                steps(pool, step)

            @block.vector
            def _(dve):
                link = Links(dve, links)

                def split(hi, lo, src):
                    link(nc.vector.tensor_copy(hi, src))
                    return nc.vector.tensor_tensor(lo, src, hi.bitcast(F32), ALU.subtract)

                dve.wait_ge(sums_set, 1)

                def step(t):
                    old, now, nxt, far = t - 1, t, t + 1, t + 2
                    if live(now) or live(nxt) or live(far):
                        wait(dve, x_squared, 1, far, 1)
                        wait(dve, y_squared, 1, now, 1)
                        wait(dve, gf_squared, 1, nxt, 1)
                        nc.vector.tensor_scalar(sums[:, OF_G:], sums[:, OF_G:], NORM_EPS ** 2, None, ALU.max)
                        link(nc.vector.tensor_scalar(sums[:, 0:OF_G], sums[:, 0:OF_G], 1.0 / D, RMS_EPS, ALU.mult, ALU.add))
                        for k in range(RSQRT_OPS):
                            link(rsqrt_op(nc, k, sums[:, :], root[:, :], root_t[:, :]))
                    if live(now):
                        wait(dve, h_T, 1, now - 1, 1)
                        for i in range(TT):
                            last = nc.vector.tensor_scalar(hn[:, i, :], y[:, i, :], root[:, OF_Y + i:OF_Y + i + 1], None, ALU.mult)
                        last.then_inc(hn_done, 1)
                    if live(far):
                        wait(dve, xn_T, 1, far - 1, 1)
                        for i in range(TT):
                            last = nc.vector.tensor_scalar(xn[:, i, :], x_t[:, i, :], root[:, OF_X + i:OF_X + i + 1], None, ALU.mult)
                        last.then_inc(x_scaled, 1)
                    if live(nxt):
                        wait(dve, dotted, 1, nxt, 1)
                        link(nc.vector.tensor_tensor(dots[:, :], dots[:, :], root[:, OF_G:], ALU.mult))
                        link(nc.vector.tensor_scalar(dots[:, :], dots[:, :], trow_b[:, D:D + 1], 1.0, ALU.mult, ALU.add))
                        link(nc.vector.tensor_scalar(mix[:, :], dots[:, :], trow_b[:, D + 1:D + 2], None, ALU.mult))
                        link(nc.vector.tensor_scalar(keep[:, :], mix[:, :], -1.0, 1.0, ALU.mult, ALU.add))
                    if live(now):
                        wait(dve, hT_out, 1, now, 1)
                        wait(dve, ffn1_done, G1, now - 1, G1)
                        split(h_h[:, :, :], h_l[:, :, :], hT[:, :, :]).then_inc(h_split, 1)
                    if live(far):
                        wait(dve, xnT_out, 1, far, 1)
                        nc.vector.tensor_copy(xnT[:, :, T:T + 3], xnT[:, :, T - 1:T].to_broadcast([P, KT, 3])).then_inc(padded, 1)
                    if live(nxt):
                        wait(dve, bl_T, 1, nxt - 1, 1)
                        nc.vector.tensor_scalar(gfs[:, 0, :], gf[:, 0, :], keep[:, 0:1], None, ALU.mult)
                        link(nc.vector.tensor_scalar(gfs[:, 1, :], gf[:, 1, :], keep[:, 1:2], None, ALU.mult))
                        for i in range(TT):
                            last = nc.vector.scalar_tensor_tensor(blend[:, i, :], trow_b[:, 0:D], mix[:, i:i + 1], gfs[:, i, :], ALU.mult, ALU.add)
                        last.then_inc(blended, 1)
                    if live(far):
                        wait(dve, folded, 1, far, 1)
                        wait(dve, pre_done, 1, far - 1, 1)
                        split(fold_h[:, :, :], fold_l[:, :, :], fold[:, :, :]).then_inc(fold_split, 1)
                    if live(old):
                        wait(dve, ffn2_done, TT, old, TT)
                        wait(dve, x_kept, 1, old, 1)
                        wait(dve, x1_out, 16, old - 1, 16)
                        nc.vector.tensor_tensor(x1[:, :, :], out_bank[:, :].rearrange("p (t d) -> p t d", t=TT), x_b2[:, :, :],
                                                ALU.add).then_inc(x1_done, 1)
                    if live(nxt):
                        wait(dve, bl_hi, 1, nxt, 1)
                        wait(dve, mrg_done, 1, nxt - 1, 1)
                        nc.vector.tensor_tensor(bl_l[:, :, :].rearrange("p k t -> p (k t)"), bl_bank[:, :],
                                                bl_h[:, :, :].rearrange("p k t -> p (k t)").bitcast(F32), ALU.subtract).then_inc(bl_lo, 1)
                    if live(far):
                        wait(dve, pre_done, 1, far, 1)
                        wait(dve, blended, 1, far - 1, 1)
                        nc.vector.tensor_tensor(gf[:, :, :].rearrange("p t d -> p (t d)"), pre_bank[:, :],
                                                gate[:, :, :].rearrange("p t d -> p (t d)"), ALU.mult).then_inc(gf_done, 1)
                        wait(dve, gf_done, 1, far, 1)
                        wait(dve, row_in, 16, far, 16)
                        for i in range(TT):
                            last = nc.vector.tensor_tensor_reduce(out=junk[:, :], in0=gf[:, i, :], in1=trow_b[:, 0:D], scale=1.0,
                                                                  scalar=0.0, op0=ALU.mult, op1=ALU.add, accum_out=dots[:, i:i + 1])
                            last.then_inc(dotted, 1) if i == TT - 1 else link(last)
                    if live(nxt):
                        wait(dve, mrg_done, 1, nxt, 1)
                        wait(dve, hn_done, 1, nxt - 1, 1)
                        nc.vector.tensor_tensor(y[:, :, :], mrg_bank[:, :].rearrange("p (t d) -> p t d", t=TT),
                                                merge_b[:, :].unsqueeze(1).to_broadcast([P, TT, D]), ALU.add).then_inc(y_done, 1)
                steps(dve, step, link, LINKS_FIRST)


LINKS_FIRST = 20


TR_FILLS = [("proj", 0, 2), ("qk", 0, 4), ("qk", 1, 5), ("qk", 2, 6), ("qk", 3, 7), ("x2", 0, 8), ("h", 0, 9), ("gates", 0, 10),
            ("qk", 4, 11), ("qk", 5, 12), ("qk", 6, 13), ("qk", 7, 14)]
TR_LAG = {"h": 2, "proj": -1, "x2": -1, "gates": -1, "qk": 1}
TR_PER = {"h": 1, "proj": 1, "x2": 1, "gates": 1, "qk": 8}
CHUNKS = [(0, 0), (0, 1), (0, 2), (0, 3), (1, 0), (1, 1), (1, 2), (1, 3), (0, 4), (0, 5), (1, 4), (1, 5)]
CHUNK_SLOTS = [12, 13, 14, 15, 0, 1, 4, 5, 6, 7, 8, 9]
AHEAD = 4
SLOTS = H
SUM_SLOT, NORM_SLOT = (1, 9), (4, 11)
SPOTS = 6
LN_SLOT = 3
QKC = 4


def attention(nc, a, banks, ident, x1_rows, hbias, cols, x2_rows, logit, out, sbuf, sems):
    s = ExitStack()
    with s:
        wq_h, wq_l = (sbuf(s, f"wqkv_{p}", [P, KT, 3 * HW], F32R) for p in "hl")
        wo_h, wo_l = (sbuf(s, f"wout_{p}", [P, HW // P, D], F32R) for p in "hl")
        wgate = sbuf(s, "wgate", [P, KT, E])

        with ExitStack() as u:
            qk_raw = sbuf(u, "qk_raw", [P, 2 * HW // P, D])
            v_raw = sbuf(u, "v_raw", [P, KT, HW])
            o_raw = sbuf(u, "o_raw", [P, HW // P, D])
            center = sbuf(u, "center", [P, P])
            loaded, centered, hi_done, lo_done, q_scaled = sems(u, "att_loaded centered att_hi att_lo q_scaled")
            flat = lambda t: t.rearrange("p k n -> p (k n)")
            with nc.Block() as block:
                @block.sync
                def _(sp):
                    for t, src in ((qk_raw[:, :, :], a["wqk"].rearrange("(m p) n -> p m n", p=P)),
                                   (center[:, :], a["center"]),
                                   (v_raw[:, :, :], a["wv"].rearrange("(k p) n -> p k n", p=P)),
                                   (o_raw[:, :, :], a["wout"].rearrange("(k p) n -> p k n", p=P)),
                                   (wgate[:, :, :], a["wgate"].rearrange("(k p) n -> p k n", p=P))):
                        sp.dma_start(t, src).then_inc(loaded, 16)

                @block.tensor
                def _(pe):
                    pe.wait_ge(loaded, 80)
                    for k in range(KT):
                        for m in range(2 * HW // P):
                            last = nc.tensor.matmul(banks[k * 4 + m // 4][:, m % 4 * P:(m % 4 + 1) * P],
                                                    qk_raw[:, m, k * P:(k + 1) * P], center[:, :], start=True, stop=True)
                            if m % 4 == 3:
                                last.then_inc(centered, 1)

                @block.scalar
                def _(act):
                    act.wait_ge(loaded, 80)
                    for k in range(KT):
                        nc.scalar.activation(wq_h[:, k, 2 * HW:], v_raw[:, k, :], ACT.Copy).then_inc(hi_done, 1)
                    nc.scalar.activation(flat(wo_h[:, :, :]), flat(o_raw[:, :, :]), ACT.Copy).then_inc(hi_done, 1)
                    for f in range(8):
                        act.wait_ge(centered, f + 1)
                        nc.scalar.activation(wq_h[:, f // 4, f % 4 * 512:(f % 4 + 1) * 512], banks[f][:, :], ACT.Copy).then_inc(hi_done, 1)

                @block.gpsimd
                def _(pool):
                    for k in range(KT):
                        pool.wait_ge(hi_done, k + 1)
                        nc.gpsimd.tensor_tensor(wq_l[:, k, 2 * HW:], v_raw[:, k, :], wq_h[:, k, 2 * HW:].bitcast(F32), ALU.subtract).then_inc(lo_done, 1)

                @block.vector
                def _(dve):
                    nc.vector.tensor_scalar(cols[:, QN_G:QN_B + 1], cols[:, QN_G:QN_B + 1], -HD ** -0.5, None, ALU.mult).then_inc(q_scaled, 1)
                    dve.wait_ge(q_scaled, 1)
                    dve.wait_ge(hi_done, 3)
                    nc.vector.tensor_tensor(flat(wo_l[:, :, :]), flat(o_raw[:, :, :]), flat(wo_h[:, :, :]).bitcast(F32), ALU.subtract).then_inc(lo_done, 1)
                    for f in range(8):
                        dve.wait_ge(hi_done, f + 4)
                        hi = wq_h[:, f // 4, f % 4 * 512:(f % 4 + 1) * 512]
                        nc.vector.tensor_tensor(wq_l[:, f // 4, f % 4 * 512:(f % 4 + 1) * 512], banks[f][:, :], hi.bitcast(F32), ALU.subtract).then_inc(lo_done, 1)

        stats = sbuf(s, "stats", [P, TT, 6])
        mean, var, rstd, vt = (sbuf(s, n, [P, TT]) for n in ("mean", "var", "rstd", "ln_t"))
        x1 = sbuf(s, "x1_t", [P, TT, D])
        aT = sbuf(s, "aT", [P, KT, T])
        a_h, a_l = (sbuf(s, f"a_{p}", [P, KT, T], F32R) for p in "hl")
        raw = sbuf(s, "raw_qk", [P, TT * QKC, 512])
        raw_sq = [sbuf(s, f"raw_sq{i}", [P, 512]) for i in range(2)]
        ssq = sbuf(s, "ssq", [P, TT, 2 * H])
        rq, rt = sbuf(s, "rq", [P, 2 * H]), sbuf(s, "rt", [P, 2 * H])
        qT = [sbuf(s, f"qT{i}", [P, H // 2, T]) for i in range(2)]
        kT = [sbuf(s, f"kT{i}", [P, H // 2, T]) for i in range(2)]
        v_h, v_l = ([sbuf(s, f"v_{p}{i}", [P, TT, H // 2, 3, HD], F32R) for i in range(2)] for p in "hl")
        shift = sbuf(s, "shift", [P, 2, TT])
        prob = [sbuf(s, f"prob{i}", [P, TT, T]) for i in range(2)]
        pT_h, pT_l = ([sbuf(s, f"pT_{p}{i}", [P, TT, T], F32R) for i in range(2)] for p in "hl")
        denom, share = sbuf(s, "denom", [P, 2, TT]), sbuf(s, "share_p", [P, 2, TT])
        o_h, o_l = (sbuf(s, f"o_{p}", [P, HW // P, T], F32R) for p in "hl")
        x2 = sbuf(s, "x2", [P, TT, D])
        proj = sbuf(s, "proj", [P, TT, D])
        x2T = proj
        tr, chunk_bank, score_bank, pT_bank, o_bank = banks[0], banks[1:3], banks[3:5], banks[5:7], banks[7]

        (zeros_set, x1_in, x1_again_in, normed_x, tr_h, tr_proj, tr_x2, tr_gates, tr_qk, out_h, out_proj, out_x2, out_gates, out_qk,
         a_hi, a_lo, chunk_done, chunk_out, v_lo, summed, rooted, normed, scored, lowest, exped, inverted, shared, pT_done, pT_hi, pT_lo,
         pv_done, o_hi, o_lo, x2_done, x2_stored, links) = sems(
            s, "zeros_set x1_in x1_again_in normed_x tr_h tr_proj tr_x2 tr_gates tr_qk out_h out_proj out_x2 out_gates out_qk "
               "a_hi a_lo chunk_done chunk_out v_lo summed rooted normed scored lowest exped inverted shared pT_done pT_hi pT_lo "
               "pv_done o_hi o_lo x2_done x2_stored att_links")
        drained = {"h": out_h, "proj": out_proj, "x2": out_x2, "gates": out_gates, "qk": out_qk}

        def tr_free(eng, t, name, j):
            at = [f[:2] for f in TR_FILLS].index((name, j))
            while True:
                at -= 1
                if at < 0:
                    at, t = at + len(TR_FILLS), t - 1
                    if isinstance(t, int) and t < -2:
                        return
                n, j, _ = TR_FILLS[at]
                b = t + TR_LAG[n]
                if live(b):
                    eng.wait_ge(drained[n], b * TR_PER[n] + j + 1)
                    return

        def steps(eng, step, link=None, per=0):
            for t in (-2, -1, 0, 1):
                step(t, t % 2)
            with eng.Fori(0, NB // 2 - 2) as i:
                if link:
                    link.enter(i, per)
                for odd in (0, 1):
                    step(i * 2 + 2 + odd, odd)
                if link:
                    link.leave(NB // 2 - 2)
            for t in range(NB - 2, NB + 1):
                step(t, t % 2)

        with nc.Block() as block:
            @block.sync
            def _(sp):
                def step(t, odd):
                    b = t + 2
                    if live(b):
                        wait(sp, tr_h, 1, b - 1, 1)
                        sp.dma_start(x1[:, :, :], x1_rows[bass.ds(b * T, T), :].rearrange("(t p) d -> p t d", p=P)).then_inc(x1_in, 16)
                    b = t - 1
                    if live(b):
                        wait(sp, tr_x2, 1, b - 1, 1)
                        sp.dma_start(x2[:, :, :], x1_rows[bass.ds(b * T, T), :].rearrange("(t p) d -> p t d", p=P)).then_inc(x1_again_in, 16)
                        wait(sp, x2_done, 1, b, 1)
                        for dst in (out, x2_rows):
                            sp.dma_start(dst[bass.ds(b * T, T), :].rearrange("(t p) d -> p t d", p=P), x2[:, :, :]).then_inc(x2_stored, 16)
                steps(sp, step)
                sp.wait_ge(x2_stored, 32 * NB)

            @block.tensor
            def _(pe):
                def step(t, odd):
                    for i in range(SLOTS):
                        if live(t):
                            hp, r = i // 2, slice(i % 2 * HD, (i % 2 + 1) * HD)
                            if i == 0:
                                wait(pe, out_qk, 8, t, 8)
                            wait(pe, exped, H, t, i - 1)
                            for n in range(TT):
                                last = nc.tensor.matmul(score_bank[i % 2][:, n * T:(n + 1) * T], qT[odd][r, hp, n * P:(n + 1) * P],
                                                        kT[odd][r, hp, :], start=True, stop=True)
                            last.then_inc(scored, 1)
                        b, j = chunk_at(t, i)
                        if j is not None and live(b):
                            n, c = CHUNKS[j]
                            if j == 0:
                                wait(pe, a_hi, 1, b, 1)
                                wait(pe, a_lo, 1, b, 1)
                            if 2 <= j < 2 + TT * QKC:
                                wait(pe, chunk_out, 12, b, j - 1)
                            else:
                                wait(pe, v_lo, 4, b, j - 1 if j < 2 else j - TT * QKC - 1)
                            product(nc, chunk_bank[j % 2][:, :],
                                    lambda k: (a_h[:, k, n * P:(n + 1) * P], a_l[:, k, n * P:(n + 1) * P]),
                                    lambda k: (wq_h[:, k, c * 512:(c + 1) * 512], wq_l[:, k, c * 512:(c + 1) * 512]),
                                    range(KT)).then_inc(chunk_done, 1)
                        b, h, _ = head_at(t, i, 1, odd)
                        if live(b):
                            wait(pe, shared, H, b, h + 1)
                            wait(pe, pT_lo, H, b, h - 1)
                            for m in range(TT):
                                for n in range(TT):
                                    last = nc.tensor.transpose(pT_bank[h % 2][:, m * T + n * P:m * T + (n + 1) * P], prob[h % 2][:, n, m * P:(m + 1) * P], ident[:, :])
                            last.then_inc(pT_done, 1)
                        b, h, its = head_at(t, i, 2, odd)
                        if live(b):
                            wait(pe, pT_lo, H, b, h + 1)
                            q = h // 2
                            if h == 0:
                                wait(pe, v_lo, 4, b, 4)
                                pe.wait_ge(zeros_set, 1)
                            if h % 2 == 0:
                                wait(pe, o_lo, H // 2, b, q)
                            x = 0
                            for m in range(TT):
                                vh, vl = (v[its][:, m, q, h % 2:h % 2 + 2, :].rearrange("p a d -> p (a d)") for v in (v_h, v_l))
                                ph, pl = (v[h % 2][:, m, :] for v in (pT_h, pT_l))
                                for l, r in ((vh, ph), (vh, pl), (vl, ph)):
                                    last = nc.tensor.matmul(o_bank[:, 0:T], l, r, start=(h % 2 == 0 and x == 0), stop=(h % 2 == 1 and x == 3 * TT - 1))
                                    x += 1
                            last.then_inc(pv_done, 1)
                        for name, j, slot in TR_FILLS:
                            b = t + TR_LAG[name]
                            if not live(b):
                                continue
                            if name == "proj" and slot <= i < slot + TT:
                                n = i - slot
                                if n == 0:
                                    wait(pe, o_lo, H // 2, b, H // 2)
                                    tr_free(pe, t, name, j)
                                last = product(nc, tr[:, n * D:(n + 1) * D],
                                               lambda k: (o_h[:, k, n * P:(n + 1) * P], o_l[:, k, n * P:(n + 1) * P]),
                                               lambda k: (wo_h[:, k, :], wo_l[:, k, :]), range(HW // P))
                                if n == TT - 1:
                                    last.then_inc(tr_proj, 1)
                            if slot != i:
                                continue
                            if name == "h":
                                wait(pe, normed_x, 1, b, 1)
                                tr_free(pe, t, name, j)
                                for k in range(KT):
                                    for n in range(TT):
                                        last = nc.tensor.transpose(tr[:, k * T + n * P:k * T + (n + 1) * P], x1[:, n, k * P:(k + 1) * P], ident[:, :])
                                last.then_inc(tr_h, 1)
                            if name == "qk":
                                wait(pe, normed, 8, b, j + 1)
                                tr_free(pe, t, name, j)
                                for m in range(4):
                                    last = nc.tensor.transpose(tr[:, m * P:(m + 1) * P], raw[:, j, m * P:(m + 1) * P], ident[:, :])
                                last.then_inc(tr_qk, 1)
                            if name == "x2":
                                wait(pe, x2_done, 1, b, 1)
                                wait(pe, x2_stored, 32, b, 32)
                                tr_free(pe, t, name, j)
                                for k in range(KT):
                                    for n in range(TT):
                                        last = nc.tensor.transpose(tr[:, k * T + n * P:k * T + (n + 1) * P], x2[:, n, k * P:(k + 1) * P], ident[:, :])
                                last.then_inc(tr_x2, 1)
                            if name == "gates":
                                wait(pe, out_x2, 1, b, 1)
                                tr_free(pe, t, name, j)
                                for n in range(TT):
                                    for k in range(KT):
                                        last = nc.tensor.matmul(tr[:, n * E:(n + 1) * E], x2T[:, k, n * P:(n + 1) * P], wgate[:, k, :],
                                                                start=(k == 0), stop=(k == KT - 1))
                                last.then_inc(tr_gates, 1)
                steps(pe, step)

            @block.scalar
            def _(act):
                def step(t, odd):
                    for i in range(SLOTS):
                        b, h, _ = head_at(t, i, 3, odd)
                        if h % 2 == 1 and live(b):
                            wait(act, pv_done, H, b, h + 1)
                            wait(act, tr_proj, 1, b - 1, 1)
                            nc.scalar.activation(o_h[:, h // 2, :], o_bank[:, 0:T], ACT.Copy).then_inc(o_hi, 1)
                        for name, j, slot in TR_FILLS:
                            b = t + TR_LAG[name]
                            if i != slot + (TT if name == "proj" else 1) or not live(b):
                                continue
                            if name == "h":
                                wait(act, tr_h, 1, b, 1)
                                wait(act, a_lo, 1, b - 1, 1)
                                for k in range(KT):
                                    last = nc.scalar.activation(aT[:, k, :], tr[:, k * T:(k + 1) * T], ACT.Identity,
                                                                bias=hbias[:, k, bass.ds(b, 1)], scale=cols[:, LN1_G + k:LN1_G + k + 1])
                                last.then_inc(out_h, 1)
                            if name == "qk":
                                wait(act, tr_qk, 8, b, j + 1)
                                dst, g = (qT, QN_G) if j % 4 < 2 else (kT, KN_G)
                                nc.scalar.activation(dst[1 - odd][:, j % 2 * 4:j % 2 * 4 + 4, j // 4 * P:(j // 4 + 1) * P],
                                                     tr[:, :].rearrange("p (m n) -> p m n", m=4), ACT.Identity,
                                                     bias=cols[:, g + 1:g + 2], scale=cols[:, g:g + 1]).then_inc(out_qk, 1)
                            if name == "proj":
                                wait(act, tr_proj, 1, b, 1)
                                wait(act, tr_gates, 1, b - 1, 1)
                                nc.scalar.activation(proj[:, :, :].rearrange("p k n -> p (k n)"), tr[:, :], ACT.Copy).then_inc(out_proj, 1)
                            if name == "x2":
                                wait(act, tr_x2, 1, b, 1)
                                nc.scalar.activation(x2T[:, :, :].rearrange("p k n -> p (k n)"), tr[:, :], ACT.Copy).then_inc(out_x2, 1)
                            if name == "gates":
                                wait(act, tr_gates, 1, b, 1)
                                nc.scalar.activation(logit[:, bass.ds(b * TT, TT), :], tr[:, 0:TT * E].rearrange("p (n e) -> p n e", n=TT), ACT.Copy).then_inc(out_gates, 1)
                        if live(t):
                            wait(act, lowest, H, t, i + 1)
                            wait(act, pT_done, H, t, i - 1)
                            for n in range(TT):
                                last = nc.scalar.activation(prob[i % 2][:, n, :], score_bank[i % 2][:, n * T:(n + 1) * T], ACT.Exp,
                                                            bias=shift[:, i % 2, n:n + 1], scale=-1.0,
                                                            accum_out=denom[:, i % 2, n:n + 1])
                            last.then_inc(exped, 1)
                        b, j = chunk_at(t, i)
                        if j is not None and live(b):
                            n, c = CHUNKS[j]
                            wait(act, chunk_done, 12, b, j + 1)
                            if c < QKC:
                                e = n * QKC + c
                                wait(act, tr_qk, 8, b - 1, e + 1)
                                nc.scalar.activation(raw[:, e, :], chunk_bank[j % 2][:, :], ACT.Copy)
                                wait(act, summed, 8, b, e - 1)
                                nc.scalar.activation(raw_sq[e % 2][:, :], chunk_bank[j % 2][:, :], ACT.Square).then_inc(chunk_out, 1)
                            else:
                                wait(act, pv_done, H, b - 2, H)
                                nc.scalar.activation(v_h[1 - odd][:, n, (c - QKC) * 4:(c - QKC + 1) * 4, 0:3:2, :],
                                                     chunk_bank[j % 2][:, :].rearrange("p (q h d) -> p q h d", q=4, h=2), ACT.Copy).then_inc(chunk_out, 1)
                        b, h, _ = head_at(t, i, 1, odd)
                        if live(b):
                            wait(act, pT_done, H, b, h + 1)
                            wait(act, pv_done, H, b, h - 1)
                            nc.scalar.activation(pT_h[h % 2][:, :, :].rearrange("p m n -> p (m n)"), pT_bank[h % 2][:, :], ACT.Copy).then_inc(pT_hi, 1)
                steps(act, step)

            @block.gpsimd
            def _(pool):
                for v in v_h + v_l:
                    last = nc.gpsimd.memset(v[:, :, :, 1, :].bitcast(F32), 0.0)
                last.then_inc(zeros_set, 1)

                def step(t, odd):
                    far, new, old = t + 2, t + 1, t - 1
                    for i in range(SLOTS):
                        for n in range(TT):
                            c = i - NORM_SLOT[n]
                            if live(new) and 0 <= c < QKC:
                                if c == 0:
                                    wait(pool, rooted, TT, new, n + 1)
                                nc.gpsimd.tensor_tensor(raw[:, n * QKC + c, :].rearrange("p (h d) -> p h d", h=8), raw[:, n * QKC + c, :].rearrange("p (h d) -> p h d", h=8),
                                                        rq[:, c * 8:(c + 1) * 8].unsqueeze(2).to_broadcast([P, 8, HD]), ALU.mult).then_inc(normed, 1)
                        if live(old) and i == 5:
                            wait(pool, out_proj, 1, old, 1)
                            wait(pool, x1_again_in, 16, old, 16)
                            nc.gpsimd.tensor_tensor(x2[:, :, :], proj[:, :, :], x2[:, :, :], ALU.add).then_inc(x2_done, 1)
                        if live(far) and i == 11:
                            wait(pool, a_hi, 1, far, 1)
                            wait(pool, chunk_done, 12, far - 1, 12)
                            nc.gpsimd.tensor_tensor(a_l[:, :, :], aT[:, :, :], a_h[:, :, :].bitcast(F32), ALU.subtract).then_inc(a_lo, 1)
                        if live(t):
                            wait(pool, inverted, H, t, i + 1)
                            nc.gpsimd.tensor_tensor(prob[i % 2][:, :, :], prob[i % 2][:, :, :],
                                                    share[:, i % 2, :].unsqueeze(2).to_broadcast([P, TT, T]), ALU.mult).then_inc(shared, 1)
                steps(pool, step)

            @block.vector
            def _(dve):
                link = Links(dve, links)

                def chains(t, i, spot):
                    new, far = t + 1, t + 2
                    for n in range(TT):
                        k = (i - SUM_SLOT[n]) * SPOTS + spot
                        if live(new) and 0 <= k <= RSQRT_OPS:
                            if k == 0:
                                wait(dve, summed, 8, new, (n + 1) * QKC)
                                link.note(nc.vector.tensor_scalar(ssq[:, n, :], ssq[:, n, :], 1.0 / HD, LN_EPS, ALU.mult, ALU.add))
                            else:
                                wait(dve, normed, 8, new, n * QKC)
                                link.settle()
                                ins = rsqrt_op(nc, k - 1, ssq[:, n, :], rq[:, :], rt[:, :])
                                ins.then_inc(rooted, 1) if k == RSQRT_OPS else link.note(ins)
                    k = (i - LN_SLOT) * SPOTS + spot
                    if live(far) and 0 <= k < TT:
                        wait(dve, x1_in, 16, far, 16)
                        link.note(nc.vector.bn_stats(stats[:, k, :], x1[:, k, :]))
                    k -= TT
                    if live(far) and 0 <= k < MOMENTS_OPS:
                        link.settle()
                        link.note(moments_op(nc, k, stats, mean[:, :], var[:, :], vt[:, :]))
                    k -= MOMENTS_OPS
                    if live(far) and 0 <= k < RSQRT_OPS:
                        link.settle()
                        link.note(rsqrt_op(nc, k, var[:, :], rstd[:, :], vt[:, :]))
                    k -= RSQRT_OPS
                    if live(far) and 0 <= k < TT:
                        link.settle()
                        ins = nc.vector.tensor_scalar(x1[:, k, :], x1[:, k, :], mean[:, k:k + 1], rstd[:, k:k + 1], ALU.subtract, ALU.mult)
                        ins.then_inc(normed_x, 1) if k == TT - 1 else link.note(ins)

                def step(t, odd):
                    far, new = t + 2, t + 1
                    for i in range(SLOTS):
                        chains(t, i, 0)
                        b, h, _ = head_at(t, i, 2, odd)
                        if live(b):
                            wait(dve, pT_hi, H, b, h + 1)
                            wait(dve, pv_done, H, b, h - 1)
                            nc.vector.tensor_tensor(pT_l[h % 2][:, :, :].rearrange("p m n -> p (m n)"), pT_bank[h % 2][:, :],
                                                    pT_h[h % 2][:, :, :].rearrange("p m n -> p (m n)").bitcast(F32), ALU.subtract).then_inc(pT_lo, 1)
                        b, h, _ = head_at(t, i, 3, odd)
                        if h % 2 == 1 and live(b):
                            wait(dve, o_hi, H // 2, b, h // 2 + 1)
                            nc.vector.tensor_tensor(o_l[:, h // 2, :], o_bank[:, 0:T], o_h[:, h // 2, :].bitcast(F32), ALU.subtract).then_inc(o_lo, 1)
                        chains(t, i, 1)
                        if live(t):
                            wait(dve, scored, H, t, i + 1)
                            wait(dve, exped, H, t, i - 1)
                            nc.vector.tensor_reduce(shift[:, i % 2, :], score_bank[i % 2][:, :].rearrange("p (n m) -> p n m", n=TT), AX, ALU.min).then_inc(lowest, 1)
                        chains(t, i, 2)
                        chains(t, i, 3)
                        b, j = chunk_at(t, i - 1)
                        if j is not None and live(b):
                            n, c = CHUNKS[j]
                            wait(dve, chunk_out, 12, b, j + 1)
                            if c < QKC:
                                nc.vector.tensor_reduce(ssq[:, n, c * 8:(c + 1) * 8], raw_sq[c % 2][:, :].rearrange("p (h d) -> p h d", h=8), AX, ALU.add).then_inc(summed, 1)
                            else:
                                nc.vector.tensor_tensor(v_l[1 - odd][:, n, (c - QKC) * 4:(c - QKC + 1) * 4, 0:3:2, :],
                                                        chunk_bank[j % 2][:, :].rearrange("p (q h d) -> p q h d", q=4, h=2),
                                                        v_h[1 - odd][:, n, (c - QKC) * 4:(c - QKC + 1) * 4, 0:3:2, :].bitcast(F32), ALU.subtract).then_inc(v_lo, 1)
                        chains(t, i, 4)
                        if live(far) and i == 10:
                            wait(dve, out_h, 1, far, 1)
                            wait(dve, chunk_done, 12, far - 1, 12)
                            nc.vector.tensor_copy(a_h[:, :, :], aT[:, :, :]).then_inc(a_hi, 1)
                        if live(t):
                            wait(dve, exped, H, t, i + 1)
                            wait(dve, shared, H, t, i - 1)
                            nc.vector.reciprocal(share[:, i % 2, :], denom[:, i % 2, :]).then_inc(inverted, 1)
                        chains(t, i, 5)
                steps(dve, step, link, LINKS_ATTENTION)


LINKS_ATTENTION = 86


def experts(nc, a, banks, ident, cols, x2_rows, logit, out, sbuf, sems):
    s = ExitStack()
    with s:
        steps32, steps16 = sbuf(s, "steps32", [P, 32]), sbuf(s, "steps16", [P, 16])
        quarter, token = sbuf(s, "quarter", [P, 4]), sbuf(s, "token", [P, TILES])
        spread = sbuf(s, "spread", [32, P], F32R)
        gates = sbuf(s, "gates", [P, TILES, E])
        gate_h, gate_l = (sbuf(s, f"gate_{p}", [P, TILES, E], F32R) for p in "hl")
        low, high = sbuf(s, "slot_low", [P, TILES, E]), sbuf(s, "slot_high", [P, TILES, E])

        with ExitStack() as u:
            peak, denom = sbuf(u, "peak", [P, TILES]), sbuf(u, "gate_sum", [P, TILES])
            tables = sbuf(u, "tables", [P, 4 * P])
            earlier, ones = (sbuf(u, n, [P, P], mybir.dt.bfloat16) for n in ("earlier", "ones_b"))
            by_expert = sbuf(u, "by_expert", [P, 2 * P])
            junk = sbuf(u, "count_junk", [P, 2 * P], mybir.dt.bfloat16)
            count = sbuf(u, "count", [P, 1])
            bit, prefix, trial, keep = (sbuf(u, n, [P, 1], I32) for n in ("bit", "prefix", "trial", "kept_bit"))
            above, tied = sbuf(u, "above", [P, 2 * P]), sbuf(u, "tied", [P, 2 * P])
            above_b, tied_b, chosen_b = (sbuf(u, n, [P, TILES, E], mybir.dt.bfloat16) for n in ("above_b", "tied_b", "chosen_b"))
            chosen, slot = sbuf(u, "chosen", [P, TILES, E]), sbuf(u, "slot", [P, TILES, E])
            slot_i, part_i = sbuf(u, "slot_i", [P, TILES, E], I32), sbuf(u, "part_i", [P, TILES, E], I32)
            flat = lambda t: t[:, :, :].rearrange("p t e -> p (t e)")
            (loaded, centred, exped, gated, tr_gates, counted, totalled, found, masked, tr_masks, masks_out, ranked, chose,
             placed, links) = sems(u, "rt_loaded rt_centred rt_exped rt_gated rt_tr_gates counted totalled found masked "
                                   "tr_masks masks_out ranked chose placed route_links")
            BITS = 30
            with nc.Block() as block:
                @block.sync
                def _(sp):
                    for t, src in ((tables[:, :], a["tables"]), (steps32[:, :], a["counts"][:, 0:32]), (steps16[:, :], a["counts"][:, 0:16]),
                                   (quarter[:, :], a["counts"][:, 32:36]), (token[:, :], a["counts"][:, 36:36 + TILES])):
                        sp.dma_start(t, src).then_inc(loaded, 16)

                @block.scalar
                def _(act):
                    act.wait_ge(centred, 1)
                    nc.scalar.activation(gates[:, :, :], gates[:, :, :], ACT.Exp).then_inc(exped, 1)

                @block.tensor
                def _(pe):
                    pe.wait_ge(gated, 1)
                    for i in range(2):
                        last = nc.tensor.transpose(banks[0][:, i * P:(i + 1) * P], flat(gates)[:, i * P:(i + 1) * P], ident[:, :])
                    last.then_inc(tr_gates, 1)
                    with pe.Fori(0, BITS) as i:
                        pe.wait_ge(counted, i + 1)
                        nc.tensor.matmul(banks[1][:, 0:1], tables[:, P:2 * P], count[:, :], start=True, stop=True).then_inc(totalled, 1)
                    pe.wait_ge(masked, 1)
                    for n, m in enumerate((above, tied)):
                        for i in range(2):
                            last = nc.tensor.transpose(banks[2 + n][:, i * P:(i + 1) * P], m[:, i * P:(i + 1) * P], ident[:, :])
                    last.then_inc(tr_masks, 1)
                    def earlier_count(bank, mask, first):
                        nc.tensor.matmul(bank[:, 0:TILES * E], earlier[:, :], flat(mask), start=True, stop=False)
                        for i in range(TILES - 1):
                            last = nc.tensor.matmul(bank[:, (i + 1) * E:TILES * E].rearrange("p (t e) -> p t e", e=E), ones[:, :],
                                                    mask[:, i:i + 1, :].to_broadcast([P, TILES - 1 - i, E]), start=False,
                                                    stop=(not first and i == TILES - 2))
                        return last
                    pe.wait_ge(masks_out, 1)
                    earlier_count(banks[4], tied_b, True)
                    for i in range(TILES):
                        last = nc.tensor.matmul(banks[4][:, 0:TILES * E].rearrange("p (t e) -> p t e", e=E), ones[:, :],
                                                above_b[:, i:i + 1, :].to_broadcast([P, TILES, E]), start=False, stop=(i == TILES - 1))
                    last.then_inc(ranked, 1)
                    pe.wait_ge(chose, 1)
                    earlier_count(banks[5], chosen_b, False).then_inc(placed, 1)

                @block.vector
                def _(dve):
                    link = Links(dve, links)
                    vec = nc.vector
                    wide = lambda t: t[:, :].unsqueeze(2).to_broadcast([P, TILES, E])
                    link(vec.reduce_max(peak[:, :], logit[:, :, :], AX))
                    vec.tensor_tensor(gates[:, :, :], logit[:, :, :], wide(peak), ALU.subtract).then_inc(centred, 1)
                    dve.wait_ge(exped, 1)
                    link(vec.tensor_reduce(denom[:, :], gates[:, :, :], AX, ALU.add))
                    link(vec.reciprocal(denom[:, :], denom[:, :]))
                    vec.tensor_tensor(gates[:, :, :], gates[:, :, :], wide(denom), ALU.mult).then_inc(gated, 1)
                    dve.wait_ge(gated, 1)
                    link(vec.tensor_copy(gate_h[:, :, :], gates[:, :, :]))
                    vec.tensor_tensor(gate_l[:, :, :], gates[:, :, :], gate_h[:, :, :].bitcast(F32), ALU.subtract)
                    dve.wait_ge(loaded, 80)
                    vec.tensor_copy(earlier[:, :], tables[:, 0:P])
                    vec.memset(ones[:, :], 1.0)
                    vec.tensor_copy(spread[:, :], tables[0:32, 2 * P:3 * P])
                    vec.memset(prefix[:, :], 0)
                    link(vec.memset(bit[:, :], 1 << (BITS - 1)))
                    dve.wait_ge(tr_gates, 1)
                    link(vec.tensor_copy(by_expert[:, :], banks[0][:, 0:2 * P]))
                    link(vec.tensor_copy(trial[:, :], bit[:, :]))
                    with dve.Fori(0, BITS) as i:
                        link.enter(i, 5)
                        vec.tensor_scalar(junk[:, :], by_expert[:, :], trial[:, :].bitcast(F32), None, ALU.is_ge, ALU.add,
                                          accum_out=count[:, :]).then_inc(counted, 1)
                        dve.wait_ge(totalled, i + 1)
                        link(vec.tensor_scalar(keep[:, :], banks[1][:, 0:1], float(CAP), -1.0, ALU.is_ge, ALU.mult))
                        link(vec.tensor_tensor(keep[:, :], keep[:, :], bit[:, :], ALU.bitwise_and))
                        link(vec.tensor_tensor(prefix[:, :], prefix[:, :], keep[:, :], ALU.bitwise_or))
                        link(vec.tensor_scalar(bit[:, :], bit[:, :], 1, None, ALU.logical_shift_right))
                        link(vec.tensor_tensor(trial[:, :], prefix[:, :], bit[:, :], ALU.bitwise_or))
                        link.leave(BITS)
                    least = prefix[:, :].bitcast(F32)
                    link(vec.tensor_scalar(above[:, :], by_expert[:, :], least, None, ALU.is_gt))
                    vec.tensor_scalar(tied[:, :], by_expert[:, :], least, None, ALU.is_equal).then_inc(masked, 1)
                    dve.wait_ge(tr_masks, 1)
                    link(vec.tensor_copy(flat(above_b), banks[2][:, 0:2 * P]))
                    vec.tensor_copy(flat(tied_b), banks[3][:, 0:2 * P]).then_inc(masks_out, 1)
                    dve.wait_ge(ranked, 1)
                    dve.wait_ge(masks_out, 1)
                    link(vec.scalar_tensor_tensor(flat(chosen), banks[4][:, 0:TILES * E], float(CAP), flat(tied_b), ALU.is_lt, ALU.mult))
                    link(vec.tensor_tensor(flat(chosen), flat(chosen), flat(above_b), ALU.add))
                    vec.tensor_copy(flat(chosen_b), flat(chosen)).then_inc(chose, 1)
                    dve.wait_ge(placed, 1)
                    link(vec.scalar_tensor_tensor(flat(slot), banks[5][:, 0:TILES * E], 1.0, flat(chosen), ALU.add, ALU.mult))
                    link(vec.tensor_scalar(flat(slot_i), flat(slot), -1.0, None, ALU.add))
                    link(vec.tensor_scalar(flat(part_i), flat(slot_i), 31, None, ALU.bitwise_and))
                    link(vec.tensor_copy(flat(low), flat(part_i)))
                    link(vec.tensor_scalar(flat(part_i), flat(slot_i), 5, None, ALU.arith_shift_right))
                    link(vec.tensor_copy(flat(high), flat(part_i)))

        b1 = sbuf(s, "b1", [P, E * G2])
        w1, w2 = sbuf(s, "ew1", [P, KT, DD]), sbuf(s, "ew2", [P, G2, D])
        w1_h, w1_l = (sbuf(s, f"ew1_{p}", [P, KT, DD], F32R) for p in "hl")
        w2_h, w2_l = (sbuf(s, f"ew2_{p}", [P, G2, D], F32R) for p in "hl")
        b2 = sbuf(s, "eb2", [P, E, D])
        in_row = sbuf(s, "in_row", [P, TILES, 32], F32R)
        in_col = sbuf(s, "in_col", [P, TILES, 16])
        record = sbuf(s, "record", [P, TILES, 3, 16], F32R)
        rec32 = sbuf(s, "rec32", [32, 48], F32R)
        picked = sbuf(s, "picked", [P, 3 * CC, 4])
        fields = sbuf(s, "fields", [P, 3, CC])
        index = [sbuf(s, f"index{i}", [P, CC], U32) for i in range(2)]
        share = [sbuf(s, f"share{i}", [P, CC]) for i in range(2)]
        gx = sbuf(s, "gx", [P, CC, D])
        stats = sbuf(s, "e_stats", [P, CC, 6])
        mean, var, rstd, vt = (sbuf(s, n, [P, CC]) for n in ("e_mean", "e_var", "e_rstd", "e_t"))
        gn = sbuf(s, "gn", [P, CC, D])
        gT = sbuf(s, "gT", [P, KT, CAP])
        g_h, g_l = (sbuf(s, f"g_{p}", [P, KT, CAP], F32R) for p in "hl")
        hid = sbuf(s, "ehid", [P, G2, CAP])
        hid_h, hid_l = (sbuf(s, f"ehid_{p}", [P, G2, CAP], F32R) for p in "hl")
        y, yw = sbuf(s, "ey", [P, CC, D]), sbuf(s, "eyw", [P, CC, D])
        idle = sbuf(s, "idle", [P, 2])
        rec_bank, tr_banks, fc1_bank, fc2_bank = banks[0], banks[1:3], banks[3:5], banks[5:7]
        (held, b1_in, w1_in, w2_in, b2_in, w1_hi, w1_lo, w2_hi, w2_lo, built, rec_done, rec_out, spread_done, indexed, gathered,
         gn_done, tr_done, gT_out, g_split, fc1_done, gelu_done, hid_hi, hid_lo, fc2_done, y_done, scattered, links) = sems(
            s, "held b1_in w1_in w2_in b2_in w1_hi w1_lo w2_hi w2_lo built rec_done rec_out spread_done indexed gathered "
               "gn_done tr_done gT_out g_split e_fc1_done e_gelu_done e_hid_hi e_hid_lo e_fc2_done y_out scattered expert_links")

        def there(e):
            return not isinstance(e, int) or 0 <= e < E

        def wait_e(eng, sem, per, e, n):
            if there(e):
                eng.wait_ge(sem, e * per + n)

        def steps(eng, step, link=None, per=0):
            step(-1, 1)
            step(0, 0)
            with eng.Fori(0, E // 2 - 1) as i:
                if link:
                    link.enter(i, per)
                for odd in (1, 0):
                    step(i * 2 + (2 - odd), odd)
                if link:
                    link.leave(E // 2 - 1)
            step(E - 1, 1)

        with nc.Block() as block:
            @block.sync
            def _(sp):
                sp.dma_start(b1[:, :], a["b1s"]).then_inc(b1_in, 16)
                sp.dma_start(b2[:, :, :], a["b2s"].unsqueeze(0).to_broadcast([P, E, D])).then_inc(b2_in, 16)

                def step(t, odd):
                    e = t + 1
                    if there(e):
                        at1, at2 = e * D, e * DD
                        if not isinstance(e, int):
                            e, at1, at2 = sp.snap(e), sp.snap(at1), sp.snap(at2)
                        wait_e(sp, w1_lo, 1, e - 1, 1)
                        sp.dma_start(w1[:, :, :], a["fc1s"][bass.ds(at1, D), :].rearrange("(k p) n -> p k n", p=P)).then_inc(w1_in, 16)
                        wait_e(sp, w2_lo, 1, e - 1, 1)
                        sp.dma_start(w2[:, :, :], a["fc2s"][bass.ds(at2, DD), :].rearrange("(k p) n -> p k n", p=P)).then_inc(w2_in, 16)
                steps(sp, step)

            @block.tensor
            def _(pe):
                def fc1(t, m):
                    wait_e(pe, fc_lo_ready, 1, t, 1)
                    wait_e(pe, g_split, 1, t, 1)
                    if m < 2:
                        wait_e(pe, gelu_done, G2, t - 1, G2 - 1 + m)
                    else:
                        wait_e(pe, gelu_done, G2, t, m - 1)
                    product(nc, fc1_bank[m % 2][:, :], lambda k: (w1_h[:, k, m * P:(m + 1) * P], w1_l[:, k, m * P:(m + 1) * P]),
                            lambda k: (g_h[:, k, :], g_l[:, k, :]), range(KT)).then_inc(fc1_done, 1)

                def fc2(t, c):
                    if c == 0:
                        wait_e(pe, w2_lo, 1, t, 1)
                        wait_e(pe, hid_hi, G2, t, G2)
                        wait_e(pe, hid_lo, G2, t, G2)
                    if c % 2 == 0:
                        wait_e(pe, y_done, CC, t - 1, c + 2)
                    product(nc, fc2_bank[c // 2][:, c % 2 * D:(c % 2 + 1) * D],
                            lambda k: (hid_h[:, k, c * P:(c + 1) * P], hid_l[:, k, c * P:(c + 1) * P]),
                            lambda k: (w2_h[:, k, :], w2_l[:, k, :]), range(G2)).then_inc(fc2_done, 1)
                fc_lo_ready = w1_lo

                def step(t, odd):
                    new = t + 1
                    if there(t):
                        for m in range(4):
                            fc1(t, m)
                    if there(new):
                        wait_e(pe, built, 1, new, 1)
                        wait_e(pe, indexed, 1, new - 1, 1)
                        for i in range(TILES):
                            last = nc.tensor.matmul(rec_bank[0:32, 0:48], in_row[:, i, :], record[:, i, :, :].rearrange("p c n -> p (c n)"),
                                                    start=(i == 0), stop=(i == TILES - 1))
                        last.then_inc(rec_done, 1)
                    if there(t):
                        for m in range(4, 6):
                            fc1(t, m)
                    if there(new):
                        wait_e(pe, rec_out, 1, new, 1)
                        nc.tensor.matmul(rec_bank[:, 64:112], spread[:, :], rec32[:, :], start=True, stop=True).then_inc(spread_done, 1)
                    if there(t):
                        for m in range(6, G2):
                            fc1(t, m)
                        for c in range(CC - 1):
                            fc2(t, c)
                    if there(new):
                        wait_e(pe, gn_done, 1, new, 1)
                        wait_e(pe, gT_out, 1, new - 1, 1)
                        for k in range(KT):
                            for c in range(CC):
                                last = nc.tensor.transpose(tr_banks[k][:, c * P:(c + 1) * P], gn[:, c, k * P:(k + 1) * P], ident[:, :])
                        last.then_inc(tr_done, 1)
                    if there(t):
                        fc2(t, CC - 1)
                steps(pe, step)

            @block.scalar
            def _(act):
                def step(t, odd):
                    new = t + 1
                    if there(t):
                        wait_e(act, w2_in, 16, t, 16)
                        wait_e(act, fc2_done, CC, t - 1, CC)
                        nc.scalar.activation(w2_h[:, :, :], w2[:, :, :], ACT.Copy).then_inc(w2_hi, 1)
                        act.wait_ge(b1_in, 16)
                        for m in range(G2):
                            wait_e(act, fc1_done, G2, t, m + 1)
                            nc.scalar.activation(hid[:, m, :], fc1_bank[m % 2][:, :], ACT.Gelu_apprx_tanh,
                                                 bias=b1[:, bass.ds(t * G2 + m, 1)]).then_inc(gelu_done, 1)
                    if there(new):
                        wait_e(act, w1_in, 16, new, 16)
                        wait_e(act, fc1_done, G2, t, G2)
                        nc.scalar.activation(w1_h[:, :, :], w1[:, :, :], ACT.Copy).then_inc(w1_hi, 1)
                        wait_e(act, tr_done, 1, new, 1)
                        wait_e(act, g_split, 1, new - 1, 1)
                        for k in range(KT):
                            last = nc.scalar.activation(gT[:, k, :], tr_banks[k][:, :], ACT.Identity,
                                                        bias=cols[:, MLP_B + k:MLP_B + k + 1], scale=cols[:, MLP_G + k:MLP_G + k + 1])
                        last.then_inc(gT_out, 1)
                steps(act, step)

            @block.gpsimd
            def _(pool):
                holds = Links(pool, held)

                def hold():
                    pool.wait_ge(held, holds.base + holds.n)
                    nc.gpsimd.tensor_tensor(idle[:, 1:2], idle[:, 0:1], idle[:, 0:1], ALU.add).then_inc(held, 1)
                    holds.n += 1

                nc.gpsimd.memset(idle[:, :], 0.0).then_inc(held, 1)
                holds.n = 1

                def step(t, odd):
                    new = t + 1
                    if there(t):
                        wait_e(pool, w2_hi, 1, t, 1)
                        nc.gpsimd.tensor_tensor(w2_l[:, :, :], w2[:, :, :], w2_h[:, :, :].bitcast(F32), ALU.subtract).then_inc(w2_lo, 1)
                    if there(new):
                        wait_e(pool, indexed, 1, new, 1)
                        wait_e(pool, gn_done, 1, new - 1, 1)
                        hold()
                        for c in range(CC):
                            nc.gpsimd.indirect_dma_start(out=gx[:, c, :], out_offset=None, in_=x2_rows,
                                                         in_offset=bass.IndirectOffsetOnAxis(ap=index[1 - odd][:, c:c + 1], axis=0)).then_inc(gathered, 16)
                        wait_e(pool, w1_hi, 1, new, 1)
                        nc.gpsimd.tensor_tensor(w1_l[:, :, :], w1[:, :, :], w1_h[:, :, :].bitcast(F32), ALU.subtract).then_inc(w1_lo, 1)
                    if there(t):
                        wait_e(pool, scattered, 16 * CC, t - 1, 16 * CC)
                        for c in range(CC):
                            wait_e(pool, y_done, CC, t, c + 1)
                            hold()
                            nc.gpsimd.indirect_dma_start(out=out, out_offset=bass.IndirectOffsetOnAxis(ap=index[odd][:, c:c + 1], axis=0),
                                                         in_=yw[:, c, :], in_offset=None, compute_op=ALU.add).then_inc(scattered, 16)
                steps(pool, step, holds, 2 * (CC + 1))
                pool.wait_ge(scattered, 16 * CC * E)

            @block.vector
            def _(dve):
                link = Links(dve, links)
                vec = nc.vector

                def hidden(t, m):
                    wait_e(dve, gelu_done, G2, t, m + 1)
                    wait_e(dve, fc2_done, CC, t - 1, CC)
                    vec.tensor_copy(hid_h[:, m, :], hid[:, m, :]).then_inc(hid_hi, 1)
                    wait_e(dve, hid_hi, G2, t, m + 1)
                    vec.tensor_tensor(hid_l[:, m, :], hid[:, m, :], hid_h[:, m, :].bitcast(F32), ALU.subtract).then_inc(hid_lo, 1)

                def weigh(t, c, odd):
                    wait_e(dve, fc2_done, CC, t, c + 2 if c % 2 == 0 else c + 1)
                    if c == 0:
                        dve.wait_ge(b2_in, 16)
                        wait_e(dve, scattered, 16 * CC, t - 1, 16 * CC)
                    link(vec.tensor_tensor(y[:, c:c + 1, :], fc2_bank[c // 2][:, c % 2 * D:(c % 2 + 1) * D].unsqueeze(1), b2[:, bass.ds(t, 1), :], ALU.add))
                    vec.tensor_scalar(yw[:, c, :], y[:, c, :], share[odd][:, c:c + 1], None, ALU.mult).then_inc(y_done, 1)

                def step(t, odd):
                    new = t + 1
                    if there(new):
                        wait_e(dve, rec_done, 1, new - 1, 1)
                        one = lambda x, n: x[:, :, bass.ds(new, 1)].to_broadcast([P, TILES, n])
                        vec.tensor_tensor(in_row[:, :, :], one(low, 32), steps32[:, :].unsqueeze(1).to_broadcast([P, TILES, 32]), ALU.is_equal)
                        link(vec.tensor_tensor(in_col[:, :, :], one(high, 16), steps16[:, :].unsqueeze(1).to_broadcast([P, TILES, 16]), ALU.is_equal))
                        vec.tensor_tensor(record[:, :, 0, :], in_col[:, :, :], token[:, :].unsqueeze(2).to_broadcast([P, TILES, 16]), ALU.mult)
                        vec.tensor_tensor(record[:, :, 1, :], in_col[:, :, :], one(gate_hf, 16), ALU.mult)
                        vec.tensor_tensor(record[:, :, 2, :], in_col[:, :, :], one(gate_lf, 16), ALU.mult).then_inc(built, 1)
                    if there(t):
                        for m in range(4):
                            hidden(t, m)
                    if there(new):
                        wait_e(dve, rec_done, 1, new, 1)
                        wait_e(dve, spread_done, 1, new - 1, 1)
                        vec.tensor_copy(rec32[:, :], rec_bank[0:32, 0:48]).then_inc(rec_out, 1)
                    if there(t):
                        for m in range(4, 6):
                            hidden(t, m)
                    if there(new):
                        wait_e(dve, spread_done, 1, new, 1)
                        link(vec.tensor_tensor(picked[:, :, :], rec_bank[:, 64:112].rearrange("p (n q) -> p n q", q=4),
                                               quarter[:, :].unsqueeze(1).to_broadcast([P, 3 * CC, 4]), ALU.mult))
                        link(vec.tensor_reduce(fields[:, :, :].rearrange("p f c -> p (f c)"), picked[:, :, :], AX, ALU.add))
                        wait_e(dve, y_done, CC, t - 1, CC)
                        link(vec.tensor_tensor(share[1 - odd][:, :], fields[:, 1, :], fields[:, 2, :], ALU.add))
                        wait_e(dve, scattered, 16 * CC, t - 1, 16 * CC)
                        vec.tensor_copy(index[1 - odd][:, :], fields[:, 0, :]).then_inc(indexed, 1)
                    if there(t):
                        for m in range(6, G2):
                            hidden(t, m)
                    if there(new):
                        wait_e(dve, gathered, 16 * CC, new, 16 * CC)
                        for c in range(CC):
                            link(vec.bn_stats(stats[:, c, :], gx[:, c, :]))
                        moments(nc, link, stats, mean[:, :], var[:, :], vt[:, :])
                        rsqrt(nc, link, var[:, :], rstd[:, :], vt[:, :])
                        wait_e(dve, tr_done, 1, new - 1, 1)
                        for c in range(CC):
                            last = vec.tensor_scalar(gn[:, c, :], gx[:, c, :], mean[:, c:c + 1], rstd[:, c:c + 1], ALU.subtract, ALU.mult)
                        last.then_inc(gn_done, 1)
                    if there(t):
                        weigh(t, 0, odd)
                        weigh(t, 1, odd)
                    if there(new):
                        wait_e(dve, gT_out, 1, new, 1)
                        wait_e(dve, fc1_done, G2, t, G2)
                        link(vec.tensor_copy(g_h[:, :, :], gT[:, :, :]))
                        vec.tensor_tensor(g_l[:, :, :], gT[:, :, :], g_h[:, :, :].bitcast(F32), ALU.subtract).then_inc(g_split, 1)
                    if there(t):
                        weigh(t, 2, odd)
                        weigh(t, 3, odd)
                gate_hf, gate_lf = gate_h[:, :, :].bitcast(F32), gate_l[:, :, :].bitcast(F32)
                steps(dve, step, link, LINKS_EXPERTS)


LINKS_EXPERTS = 54


def tables():
    r = np.arange(P)
    t = [r[:, None] < r[None, :], r[:, None] % E == r[None, :] % E, r[:, None] == r[None, :] % 32, r[:, None] < 0 * r[None, :]]
    return np.concatenate(t, 1).astype(np.float32)


def counts():
    r = np.arange(P)[:, None]
    t = [np.broadcast_to(np.arange(32), (P, 32)), r // 32 == np.arange(4)[None, :], r + P * np.arange(TILES)[None, :]]
    return np.concatenate(t, 1).astype(np.float32)


def laid_out(v):
    f = lambda n: np.asarray(v[n])
    c = np.ascontiguousarray
    pos = (np.arange(T) / max(1, T - 1)).astype(np.float32)
    ang = np.float32(2.0 * np.pi) * pos[:, None] * np.arange(1, 9, dtype=np.float32)[None, :]
    harm = np.stack([np.sin(ang), np.cos(ang)], -1).reshape(T, 16).astype(np.float32)
    halves = lambda n: [f(n)[k * P:(k + 1) * P] for k in range(f(n).shape[0] // P)]
    twice = lambda n: [np.concatenate([f(n), f(n)])]
    cols = np.stack(halves("L0_cond_norm_in_w") + halves("L0_cond_norm_out_w") + halves("L1_cond_ln1_g")
                    + halves("L1_cond_ln1_b") + halves("L1_cond_b_ada") + halves("L1_cond_mlp_g") + halves("L1_cond_mlp_b")
                    + twice("L1_cond_qn_g") + twice("L1_cond_qn_b") + twice("L1_cond_kn_g") + twice("L1_cond_kn_b")
                    + halves("L0_cond_ffn_b1"), 1)
    cols = np.concatenate([cols, np.zeros((P, 30 - cols.shape[1]), cols.dtype)], 1)
    x = f("x")
    return {
        "x": c(x.reshape(TOKENS, D)), "xT": c(x.transpose(0, 2, 1).reshape(NB * D, T)),
        "cond": c(f("cond_1024").T), "cfg": c(f("condB_cfgscale").reshape(NB, 1)), "cols": c(cols),
        "ident": np.eye(P, dtype=np.float32), "harm": c(harm.T),
        "pre_w": c(f("L0_cond_pre_w").T), "harm_w": c(f("L0_cond_harm_w").T), "harm_b": c(f("L0_cond_harm_b")),
        "style_w": c(f("L0_cond_style_w").T), "merge_w": c(f("L0_cond_merge_w").T), "merge_b": c(f("L0_cond_merge_b")),
        "ffn_w1": c(f("L0_cond_ffn_w1").T), "ffn_w2": c(f("L0_cond_ffn_w2").T), "ffn_b2": c(f("L0_cond_ffn_b2")),
        "W_ada": c(f("L1_cond_W_ada").T),
        "wqk": c(f("L1_cond_Wqkv")[:2 * HW]), "wv": c(f("L1_cond_Wqkv")[2 * HW:].T), "wout": c(f("L1_cond_Wout").T),
        "wgate": c(f("L1_cond_Wgate").T),
        "tables": tables(), "counts": counts(), "b1s": c(f("L1_cond_b1s").reshape(E * G2, P).T), "b2s": c(f("L1_cond_b2s")),
        "fc1s": c(f("L1_cond_fc1s").transpose(0, 2, 1).reshape(E * D, DD)),
        "fc2s": c(f("L1_cond_fc2s").transpose(0, 2, 1).reshape(E * DD, D)),
        "center": np.kron(np.eye(2), np.eye(HD) - np.ones((HD, HD)) / HD).astype(np.float32),
    }


_ORDER = ["x", "xT", "cond", "cfg", "cols", "ident", "harm", "pre_w", "harm_w", "harm_b", "style_w", "merge_w", "merge_b",
          "ffn_w1", "ffn_w2", "ffn_b2", "W_ada", "wqk", "wv", "wout", "wgate", "center", "tables", "counts", "b1s", "b2s",
          "fc1s", "fc2s"]


def kernel(**inputs):
    import concourse.bacc as bacc
    from concourse.bass_utils import run_bass_kernel_spmd

    nc = bacc.Bacc("TRN2", target_bir_lowering=False, num_devices=1)
    laid = laid_out(inputs)
    arrays, args = {}, {}
    for name in _ORDER:
        arrays["in_" + name] = laid[name]
        args[name] = nc.dram_tensor("in_" + name, laid[name].shape, mybir.dt.from_np(laid[name].dtype), kind="ExternalInput").ap()
    out = nc.dram_tensor("out", (TOKENS, D), F32, kind="ExternalOutput").ap()
    build(nc, args, out)
    result = run_bass_kernel_spmd(nc, [arrays], core_ids=[0])
    return result.results[0]["out"].reshape(NB, T, D)
```

```python
from contextlib import ExitStack

import numpy as np

import concourse.bass as bass
from concourse import mybir

F32 = mybir.dt.float32
F32R = mybir.dt.float32r
I32 = mybir.dt.int32
U32 = mybir.dt.uint32
ALU = mybir.AluOpType
ACT = mybir.ActivationFunctionType
AX = mybir.AxisListType.X

P = 128
NB, T, D = 16, 256, 256
TT, KT = T // P, D // P
TOKENS = NB * T
TILES = TOKENS // P
F1 = 1024
G1 = F1 // (2 * P)
H, HD = 16, 64
HW = H * HD
E, DD = 8, 1024
CAP = TOKENS // E
CC = CAP // P
G2 = DD // P
RMS_EPS, LN_EPS, NORM_EPS = 1e-6, 1e-5, 1e-12
MAGIC = 0x5F3759DF


def live(b):
    return not isinstance(b, int) or 0 <= b < NB


def wait(eng, sem, per, b, n):
    if n <= 0:
        b, n = b - 1, n + per
    if live(b):
        eng.wait_ge(sem, b * per + n)


def head_at(t, i, lag, odd):
    return (t, i - lag, odd) if i >= lag else (t - 1, i - lag + H, 1 - odd)


def chunk_at(t, i):
    if i < 0:
        t, i = t - 1, i + SLOTS
    if i not in CHUNK_SLOTS:
        return t, None
    j = CHUNK_SLOTS.index(i)
    return (t + 2 if j < AHEAD else t + 1), j


class Links:

    def __init__(self, eng, sem):
        self.eng, self.sem, self.base, self.n = eng, sem, 0, 0

    def __call__(self, ins):
        ins.then_inc(self.sem, 1)
        self.n += 1
        self.eng.wait_ge(self.sem, self.base + self.n)

    def settle(self):
        self.eng.wait_ge(self.sem, self.base + self.n)

    def note(self, ins):
        ins.then_inc(self.sem, 1)
        self.n += 1

    def enter(self, i, per):
        self.before = self.base + self.n
        self.base, self.n, self.per = self.before + i * per, 0, per

    def leave(self, count):
        assert self.n == self.per, f"the loop's body has {self.n} links"
        self.base, self.n = self.before + count * self.per, 0


RSQRT_OPS, MOMENTS_OPS = 11, 7


def rsqrt_op(nc, k, v, y, t):
    vec = nc.vector
    if k == 0:
        return vec.tensor_scalar(t.bitcast(I32), v.bitcast(I32), 1, None, ALU.logical_shift_right)
    if k == 1:
        return vec.tensor_scalar(y.bitcast(I32), t.bitcast(I32), -1.0, float(MAGIC), ALU.mult, ALU.add)
    if k % 3 == 2:
        return vec.tensor_tensor(t, y, y, ALU.mult)
    if k % 3 == 0:
        return vec.scalar_tensor_tensor(t, t, -0.5, v, ALU.mult, ALU.mult)
    return vec.scalar_tensor_tensor(y, t, 1.5, y, ALU.add, ALU.mult)


def moments_op(nc, k, stats, mean, var, d):
    vec = nc.vector
    if k == 0:
        return vec.tensor_tensor(d, stats[:, :, 1], stats[:, :, 4], ALU.subtract)
    if k == 1:
        return vec.tensor_tensor(mean, stats[:, :, 1], stats[:, :, 4], ALU.add)
    if k == 2:
        return vec.tensor_tensor(var, stats[:, :, 2], stats[:, :, 5], ALU.add)
    if k == 3:
        return vec.tensor_tensor(d, d, d, ALU.mult)
    if k == 4:
        return vec.tensor_scalar(mean, mean, 0.5, None, ALU.mult)
    if k == 5:
        return vec.tensor_scalar(var, var, 1.0 / D, LN_EPS, ALU.mult, ALU.add)
    return vec.scalar_tensor_tensor(var, d, 0.25, var, ALU.mult, ALU.add)


def rsqrt(nc, link, v, y, t):
    for k in range(RSQRT_OPS):
        link(rsqrt_op(nc, k, v, y, t))


def moments(nc, link, stats, mean, var, d):
    for k in range(MOMENTS_OPS):
        ins = moments_op(nc, k, stats, mean, var, d)
        if k in (2, 5, 6):
            link(ins)


def product(nc, out, lhs, rhs, ks):
    n = 0
    for k in ks:
        (ah, al), (bh, bl) = lhs(k), rhs(k)
        for a, b in ((ah, bh), (ah, bl), (al, bh)):
            last = nc.tensor.matmul(out, a, b, start=(n == 0), stop=(n == 3 * len(ks) - 1))
            n += 1
    return last


def build(nc, a, out):
    top = ExitStack()
    with top:
        def sbuf(stack, name, shape, dt=F32):
            return stack.enter_context(nc.sbuf_tensor(name, shape, dt))

        def sems(stack, names):
            return [stack.enter_context(nc.semaphore(n)) for n in names.split()]

        banks = [top.enter_context(nc.psum_tensor(f"bank{i}", [P, 512], F32)) for i in range(8)]
        ident = sbuf(top, "ident", [P, P])
        hbias = sbuf(top, "hbias", [P, KT, NB])
        cols = sbuf(top, "cols", [P, 30])
        x1_rows = nc.dram_tensor("x1_rows", [TOKENS, D], F32).ap()
        target_rows = nc.dram_tensor("target_rows", [NB, D + 2], F32).ap()
        x2_rows = nc.dram_tensor("x2_rows", [TOKENS, D], F32).ap()
        logit = sbuf(top, "logit", [P, TILES, E])

        landing, center, wgate = sbuf(top, "landing", [P, 4, H // 2 * T]), sbuf(top, "center", [P, P]), sbuf(top, "wgate", [P, KT, E])
        qk_raw = landing[:, 0:2, :].rearrange("p i (m n) -> p (i m) n", n=D)
        v_raw = landing[:, 2, :].rearrange("p (k n) -> p k n", k=KT)
        o_raw = landing[:, 3, :].rearrange("p (k n) -> p k n", n=D)
        att_loaded, = sems(top, "att_loaded")

        def load_attention(sp):
            for t, src in ((qk_raw, a["wqk"].rearrange("(m p) n -> p m n", p=P)), (center[:, :], a["center"]),
                           (v_raw, a["wv"].rearrange("(k p) n -> p k n", p=P)), (o_raw, a["wout"].rearrange("(k p) n -> p k n", p=P)),
                           (wgate[:, :, :], a["wgate"].rearrange("(k p) n -> p k n", p=P))):
                sp.dma_start(t, src).then_inc(att_loaded, 16)

        first_block(nc, a, banks, ident, x1_rows, hbias, cols, target_rows, load_attention, sbuf, sems)
        attention(nc, (landing, qk_raw, v_raw, o_raw, center, wgate, att_loaded), banks, ident, x1_rows, hbias, cols, x2_rows, logit,
                  out, sbuf, sems)
        experts(nc, a, banks, ident, cols, x2_rows, logit, out, sbuf, sems)


NORM_IN, NORM_OUT, LN1_G, LN1_B, B_ADA, MLP_G, MLP_B = (0, 2, 4, 6, 8, 10, 12)
QN_G, QN_B, KN_G, KN_B = (14, 15, 16, 17)
FFN_B1 = 18


def first_block(nc, a, banks, ident, x1_rows, hbias, cols, target_rows, load_attention, sbuf, sems):
    s = ExitStack()
    with s:
        pre_h, pre_l = (sbuf(s, f"pre_{p}", [P, KT, D], F32R) for p in "hl")
        mrg_h, mrg_l = (sbuf(s, f"mrg_{p}", [P, 2 * KT, D], F32R) for p in "hl")
        w1_h, w1_l = (sbuf(s, f"w1_{p}", [P, KT, F1], F32R) for p in "hl")
        w2_h, w2_l = (sbuf(s, f"w2_{p}", [P, F1 // P, D], F32R) for p in "hl")
        gate = sbuf(s, "gate", [P, TT, D])
        merge_b, ffn_b2 = sbuf(s, "merge_b", [P, D]), sbuf(s, "ffn_b2", [P, D])

        with ExitStack() as u:
            raw = sbuf(u, "raw", [P, 5632])
            cond_t, silu_t = sbuf(u, "cond_t", [P, KT, NB]), sbuf(u, "silu_t", [P, KT, NB])
            style_w, ada_w = sbuf(u, "style_w", [P, KT, D]), sbuf(u, "ada_w", [P, KT, D])
            harm, harm_w = sbuf(u, "harm", [16, T]), sbuf(u, "harm_w", [16, D])
            harm_b = sbuf(u, "harm_b", [P, D])
            trow = sbuf(u, "trow", [NB, D + 2])
            tsq, tss, tmp = sbuf(u, "tsq", [NB, D]), sbuf(u, "tss", [NB, 1]), sbuf(u, "tmp", [NB, 1])
            cfg = sbuf(u, "cfg", [NB, 1])
            (consts_in, vectors_in, hi_done, lo_done, silu_done, style_done, target_done,
             ada_done, hbias_done, harm_done, gate_sum, gate_done, target_sq, links, row_done,
             row_out) = sems(u, "consts_in vectors_in hi_done lo_done silu_done "
                             "style_done target_done ada_done hbias_done harm_done gate_sum "
                             "gate_done target_sq setup_links row_done row_out")
            weights_in = sems(u, "pre_w_in merge_w_in ffn_w1_in ffn_w2_in")
            pieces = [(pre_h, pre_l, 0, KT * D, a["pre_w"], KT), (mrg_h, mrg_l, 512, 2 * KT * D, a["merge_w"], 2 * KT),
                      (w1_h, w1_l, 1536, KT * F1, a["ffn_w1"], KT), (w2_h, w2_l, 3584, F1 // P * D, a["ffn_w2"], F1 // P)]

            def low_part(eng, i):
                hi, lo, at, n, _, _ = pieces[i]
                return eng.tensor_tensor(lo[:, :, :].rearrange("p k n -> p (k n)"), raw[:, at:at + n],
                                         hi[:, :, :].rearrange("p k n -> p (k n)").bitcast(F32), ALU.subtract)

            with nc.Block() as block:
                @block.sync
                def _(sp):
                    for t, src in ((ident[:, :], a["ident"]), (harm[:, :], a["harm"]), (harm_w[:, :], a["harm_w"]),
                                   (harm_b[:, :], a["harm_b"].unsqueeze(0).to_broadcast([P, D])),
                                   (cond_t[:, :, :], a["cond"].rearrange("(k p) b -> p k b", p=P)),
                                   (style_w[:, :, :], a["style_w"].rearrange("(k p) n -> p k n", p=P)),
                                   (ada_w[:, :, :], a["W_ada"].rearrange("(k p) n -> p k n", p=P)),
                                   (cfg[:, :], a["cfg"])):
                        sp.dma_start(t, src).then_inc(consts_in, 16)
                    load_attention(sp)
                    sp.wait_ge(row_done, 1)
                    sp.dma_start(target_rows, trow[:, :]).then_inc(row_out, 16)
                    sp.wait_ge(row_out, 16)

                @block.scalar
                def _(act):
                    for (_, _, at, n, src, k), arrived in zip(pieces, weights_in):
                        act.dma_start(raw[:, at:at + n].rearrange("p (k n) -> p k n", k=k),
                                      src.rearrange("(k p) n -> p k n", p=P)).then_inc(arrived, 16)
                    act.dma_start(cols[:, :], a["cols"]).then_inc(vectors_in, 16)
                    act.dma_start(merge_b[:, :], a["merge_b"].unsqueeze(0).to_broadcast([P, D])).then_inc(vectors_in, 16)
                    act.dma_start(ffn_b2[:, :], a["ffn_b2"].unsqueeze(0).to_broadcast([P, D])).then_inc(vectors_in, 16)
                    act.wait_ge(consts_in, 16 * 8)
                    nc.scalar.activation(silu_t[:, :, :], cond_t[:, :, :], ACT.Silu).then_inc(silu_done, 1)
                    act.wait_ge(style_done, 1)
                    nc.scalar.activation(tsq[:, :], banks[0][0:NB, 0:D], ACT.Square, accum_out=tss[:, :]).then_inc(target_sq, 1)
                    for (hi, _, at, n, _, _), arrived in zip(pieces, weights_in):
                        act.wait_ge(arrived, 16)
                        nc.scalar.activation(hi[:, :, :].rearrange("p k n -> p (k n)"), raw[:, at:at + n], ACT.Copy).then_inc(hi_done, 1)
                    act.wait_ge(gate_sum, 1)
                    nc.scalar.activation(gate[:, :, :], gate[:, :, :], ACT.Sigmoid).then_inc(gate_done, 1)
                    act.wait_ge(vectors_in, 48)

                @block.gpsimd
                def _(pool):
                    for i in range(2):
                        pool.wait_ge(hi_done, i + 1)
                        low_part(nc.gpsimd, i).then_inc(lo_done, 1)

                @block.tensor
                def _(pe):
                    pe.wait_ge(consts_in, 16 * 8)
                    for k in range(KT):
                        last = nc.tensor.matmul(banks[0][0:NB, 0:D], cond_t[:, k, :], style_w[:, k, :],
                                                start=(k == 0), stop=(k == KT - 1))
                    last.then_inc(style_done, 1)
                    for t in range(TT):
                        last = nc.tensor.matmul(banks[1][:, t * D:(t + 1) * D], harm[:, t * P:(t + 1) * P], harm_w[:, :],
                                                start=True, stop=True)
                    last.then_inc(harm_done, 1)
                    pe.wait_ge(silu_done, 1)
                    for m in range(KT):
                        for k in range(KT):
                            last = nc.tensor.matmul(banks[2][:, m * NB:(m + 1) * NB], ada_w[:, k, m * P:(m + 1) * P],
                                                    silu_t[:, k, :], start=(k == 0), stop=(k == KT - 1))
                    last.then_inc(ada_done, 1)

                @block.vector
                def _(dve):
                    link = Links(dve, links)
                    dve.wait_ge(consts_in, 16 * 8)
                    dve.wait_ge(vectors_in, 48)
                    link(nc.vector.tensor_scalar(cfg[:, :], cfg[:, :], 2.0, -2.0, ALU.min, ALU.max))
                    link(nc.vector.tensor_scalar(trow[:, D + 1:D + 2], cfg[:, :], 0.5, None, ALU.mult))
                    dve.wait_ge(target_sq, 1)
                    link(nc.vector.tensor_copy(trow[:, 0:D], banks[0][0:NB, 0:D]))
                    link(nc.vector.tensor_scalar(tss[:, :], tss[:, :], NORM_EPS ** 2, None, ALU.max))
                    rsqrt(nc, link, tss[:, :], trow[:, D:D + 1], tmp[:, :])
                    nc.vector.tensor_copy(cfg[:, :], cfg[:, :]).then_inc(row_done, 1)
                    dve.wait_ge(ada_done, 1)
                    for m in range(KT):
                        link(nc.vector.tensor_scalar(hbias[:, m, :], banks[2][:, m * NB:(m + 1) * NB],
                                                     cols[:, LN1_B + m:LN1_B + m + 1], cols[:, B_ADA + m:B_ADA + m + 1],
                                                     ALU.add, ALU.add))
                    dve.wait_ge(harm_done, 1)
                    for t in range(TT):
                        last = nc.vector.tensor_tensor(gate[:, t, :], banks[1][:, t * D:(t + 1) * D], harm_b[:, :], ALU.add)
                    last.then_inc(gate_sum, 1)
                    for i in (2, 3):
                        dve.wait_ge(hi_done, i + 1)
                        low_part(nc.vector, i).then_inc(lo_done, 1)
                    dve.wait_ge(gate_done, 1)
                    link(nc.vector.tensor_scalar(gate[:, :, :], gate[:, :, :], 0.25, None, ALU.mult))

        x_again, x_b2, x1 = (sbuf(s, n, [P, TT, D]) for n in ("x_again", "x_b2", "x1"))
        x_t = sbuf(s, "x_t", [P, TT, D])
        xT = sbuf(s, "xT", [P, KT, T])
        xT_h, xT_l = (sbuf(s, f"xT_{p}", [P, KT, T], F32R) for p in "hl")
        trow_b = sbuf(s, "trow_b", [P, D + 2])
        junk_act, junk = sbuf(s, "junk_act", [P, 3 * TT, D]), sbuf(s, "junk", [P, D])
        sums, root, root_t = (sbuf(s, n, [P, 3 * TT]) for n in ("sums", "root", "root_t"))
        OF_X, OF_Y, OF_G = 0, TT, 2 * TT
        dots, mix, keep = (sbuf(s, n, [P, TT]) for n in ("dots", "mix", "keep"))
        xn = sbuf(s, "xn", [P, TT, D])
        xnT = sbuf(s, "xnT", [P, KT, T + 3])
        pair = sbuf(s, "pair", [P, KT, T + 2])
        fold = sbuf(s, "fold", [P, KT, T])
        fold_h, fold_l = (sbuf(s, f"fold_{p}", [P, KT, T], F32R) for p in "hl")
        gf = sbuf(s, "gf", [P, TT, D])
        gfs = sbuf(s, "gfs", [P, TT, D])
        blend = sbuf(s, "blend", [P, TT, D])
        bl_h, bl_l = (sbuf(s, f"bl_{p}", [P, KT, T], F32R) for p in "hl")
        y = sbuf(s, "y", [P, TT, D])
        hn = sbuf(s, "hn", [P, TT, D])
        hT = sbuf(s, "hT", [P, KT, T])
        h_h, h_l = (sbuf(s, f"h_{p}", [P, KT, T], F32R) for p in "hl")
        hid = sbuf(s, "hid", [P, F1 // P, T])
        hid_h, hid_l = (sbuf(s, f"hid_{p}", [P, F1 // P, T], F32R) for p in "hl")
        xn_bank, pre_bank, mrg_bank, out_bank, hn_bank, bl_bank = banks[0], banks[1], banks[2], banks[3], banks[6], banks[7]
        ffn_bank = banks[4:6]

        (sums_set, x_in, xT_in, row_in, x_squared, x_scaled, x_kept, xn_T, xnT_out, padded, paired, folded, fold_split,
         pre_done, gf_done, gf_squared, dotted, blended, bl_T, bl_hi, bl_lo, xT_hi, xT_lo, mrg_done, y_done, y_squared,
         hn_done, h_T, hT_out, h_split, ffn1_done, gelu_done, hid_hi, hid_lo, ffn2_done, x1_done, x_again_in, x1_out,
         links) = sems(s, "sums_set x_in xT_in row_in x_squared x_scaled x_kept xn_T xnT_out padded paired folded fold_split "
                       "pre_done gf_done gf_squared dotted blended bl_T bl_hi bl_lo xT_hi xT_lo mrg_done y_done y_squared "
                       "hn_done h_T hT_out h_split ffn1_done gelu_done hid_hi hid_lo ffn2_done x1_done x_again_in x1_out "
                       "first_links")
        FIRST, LOOP, LAST = -3, 2, NB
        LOOPS = NB - 3 - LOOP

        def steps(eng, step, link=None, per=0):
            for t in range(FIRST, LOOP):
                step(t)
            with eng.Fori(0, LOOPS) as i:
                if link:
                    link.enter(i, per)
                step(i + LOOP)
                if link:
                    link.leave(LOOPS)
            for t in range(NB - 3, LAST + 1):
                step(t)

        with nc.Block() as block:
            @block.sync
            def _(sp):
                def step(t):
                    b = t + 3
                    if live(b):
                        wait(sp, x_scaled, 1, b - 1, 1)
                        sp.dma_start(x_t[:, :, :], a["x"][bass.ds(b * T, T), :].rearrange("(t p) d -> p t d", p=P)).then_inc(x_in, 16)
                    b = t + 2
                    if live(b):
                        wait(sp, blended, 1, b - 1, 1)
                        sp.dma_start(trow_b[:, :], target_rows[bass.ds(b, 1), :].to_broadcast([P, D + 2])).then_inc(row_in, 16)
                        wait(sp, xT_lo, 1, b - 1, 1)
                        sp.dma_start(xT[:, :, :], a["xT"][bass.ds(b * D, D), :].rearrange("(k p) t -> p k t", p=P)).then_inc(xT_in, 16)
                    b = t - 1
                    if live(b):
                        wait(sp, x1_done, 1, b, 1)
                        sp.dma_start(x1_rows[bass.ds(b * T, T), :].rearrange("(t p) d -> p t d", p=P), x1[:, :, :]).then_inc(x1_out, 16)
                    b = t
                    if live(b):
                        wait(sp, x_kept, 1, b - 1, 1)
                        sp.dma_start(x_again[:, :, :], a["x"][bass.ds(b * T, T), :].rearrange("(t p) d -> p t d", p=P)).then_inc(x_again_in, 16)
                steps(sp, step)
                sp.wait_ge(x1_out, 16 * NB)

            @block.tensor
            def _(pe):
                def transposes(bank, src):
                    for k in range(KT):
                        for t in range(TT):
                            last = nc.tensor.transpose(bank[:, k * T + t * P:k * T + (t + 1) * P], src[:, t, k * P:(k + 1) * P], ident[:, :])
                    return last

                def pre(b):
                    wait(pe, fold_split, 1, b, 1)
                    wait(pe, gf_done, 1, b - 1, 1)
                    for t in range(TT):
                        last = product(nc, pre_bank[:, t * D:(t + 1) * D],
                                       lambda k: (fold_h[:, k, t * P:(t + 1) * P], fold_l[:, k, t * P:(t + 1) * P]),
                                       lambda k: (pre_h[:, k, :], pre_l[:, k, :]), range(KT))
                    last.then_inc(pre_done, 1)

                def ffn1(b, g):
                    wait(pe, h_split, 1, b, 1)
                    wait(pe, gelu_done, G1, b, g - 1)
                    for m in (2 * g, 2 * g + 1):
                        last = product(nc, ffn_bank[g % 2][:, m % 2 * T:(m % 2 + 1) * T],
                                       lambda k: (w1_h[:, k, m * P:(m + 1) * P], w1_l[:, k, m * P:(m + 1) * P]),
                                       lambda k: (h_h[:, k, :], h_l[:, k, :]), range(KT))
                    last.then_inc(ffn1_done, 1)

                def ffn2(b, t):
                    def hidden(k):
                        if t == 0 and k % 2 == 0:
                            wait(pe, hid_lo, G1, b, k // 2 + 1)
                        return hid_h[:, k, t * P:(t + 1) * P], hid_l[:, k, t * P:(t + 1) * P]
                    wait(pe, x1_done, 1, b - 1, 1)
                    product(nc, out_bank[:, t * D:(t + 1) * D], hidden,
                            lambda k: (w2_h[:, k, :], w2_l[:, k, :]), range(F1 // P)).then_inc(ffn2_done, 1)

                def merge(b):
                    wait(pe, bl_lo, 1, b, 1)
                    wait(pe, xT_lo, 1, b, 1)
                    wait(pe, y_done, 1, b - 1, 1)
                    for t in range(TT):
                        def parts(k):
                            hi, lo = (xT_h, xT_l) if k < KT else (bl_h, bl_l)
                            return hi[:, k % KT, t * P:(t + 1) * P], lo[:, k % KT, t * P:(t + 1) * P]
                        last = product(nc, mrg_bank[:, t * D:(t + 1) * D], parts,
                                       lambda k: (mrg_h[:, k, :], mrg_l[:, k, :]), range(2 * KT))
                    last.then_inc(mrg_done, 1)

                def step(t):
                    old, now, nxt, far = t - 1, t, t + 1, t + 2
                    if live(far):
                        wait(pe, x_scaled, 1, far, 1)
                        wait(pe, xnT_out, 1, far - 1, 1)
                        transposes(xn_bank, xn).then_inc(xn_T, 1)
                    if live(now):
                        wait(pe, hn_done, 1, now, 1)
                        wait(pe, hT_out, 1, now - 1, 1)
                        transposes(hn_bank, hn).then_inc(h_T, 1)
                    if live(old):
                        ffn2(old, 0)
                    if live(nxt):
                        wait(pe, blended, 1, nxt, 1)
                        wait(pe, bl_lo, 1, nxt - 1, 1)
                        transposes(bl_bank, blend).then_inc(bl_T, 1)
                    if live(old):
                        ffn2(old, 1)
                    if live(far):
                        pre(far)
                    if live(nxt):
                        merge(nxt)
                    if live(now):
                        for g in range(G1):
                            ffn1(now, g)
                steps(pe, step)

            @block.scalar
            def _(act):
                def gelu(b, g):
                    wait(act, ffn1_done, G1, b, g + 1)
                    wait(act, ffn2_done, TT, b - 1, TT)
                    wait(act, hid_lo, G1, b - 1, G1)
                    for m in (2 * g, 2 * g + 1):
                        last = nc.scalar.activation(hid[:, m, :], ffn_bank[g % 2][:, m % 2 * T:(m % 2 + 1) * T], ACT.Gelu,
                                                    bias=cols[:, FFN_B1 + m:FFN_B1 + m + 1])
                    last.then_inc(gelu_done, 1)
                    wait(act, gelu_done, G1, b, g + 1)
                    nc.scalar.activation(hid_h[:, 2 * g:2 * g + 2, :], hid[:, 2 * g:2 * g + 2, :], ACT.Copy).then_inc(hid_hi, 1)

                def squares(src, at):
                    for i in range(TT):
                        last = nc.scalar.activation(junk_act[:, at + i, :], src[:, i, :], ACT.Square, accum_out=sums[:, at + i:at + i + 1])
                    return last

                act.wait_ge(sums_set, 1)

                def step(t):
                    now, nxt, far, new = t, t + 1, t + 2, t + 3
                    if live(far):
                        wait(act, xn_T, 1, far, 1)
                        wait(act, folded, 1, far - 1, 1)
                        for k in range(KT):
                            last = nc.scalar.activation(xnT[:, k, 0:T], xn_bank[:, k * T:(k + 1) * T], ACT.Copy,
                                                        scale=cols[:, NORM_IN + k:NORM_IN + k + 1])
                        last.then_inc(xnT_out, 1)
                    if live(now):
                        wait(act, h_T, 1, now, 1)
                        wait(act, h_split, 1, now - 1, 1)
                        for k in range(KT):
                            last = nc.scalar.activation(hT[:, k, :], hn_bank[:, k * T:(k + 1) * T], ACT.Copy,
                                                        scale=cols[:, NORM_OUT + k:NORM_OUT + k + 1])
                        last.then_inc(hT_out, 1)
                    if live(nxt):
                        wait(act, xT_in, 16, nxt, 16)
                        wait(act, mrg_done, 1, nxt - 1, 1)
                        nc.scalar.activation(xT_h[:, :, :], xT[:, :, :], ACT.Copy).then_inc(xT_hi, 1)
                    if live(nxt):
                        wait(act, bl_T, 1, nxt, 1)
                        nc.scalar.activation(bl_h[:, :, :].rearrange("p k t -> p (k t)"), bl_bank[:, :], ACT.Copy).then_inc(bl_hi, 1)
                    if live(new):
                        wait(act, x_in, 16, new, 16)
                        wait(act, x_scaled, 1, new - 1, 1)
                        squares(x_t, OF_X).then_inc(x_squared, 1)
                    if live(far):
                        wait(act, gf_done, 1, far, 1)
                        squares(gf, OF_G).then_inc(gf_squared, 1)
                    if live(nxt):
                        wait(act, y_done, 1, nxt, 1)
                        squares(y, OF_Y).then_inc(y_squared, 1)
                    if live(now):
                        for g in range(G1):
                            gelu(now, g)
                steps(act, step)

            @block.gpsimd
            def _(pool):
                def hidden_low(b, g):
                    wait(pool, hid_hi, G1, b, g + 1)
                    nc.gpsimd.tensor_tensor(hid_l[:, 2 * g:2 * g + 2, :], hid[:, 2 * g:2 * g + 2, :],
                                            hid_h[:, 2 * g:2 * g + 2, :].bitcast(F32), ALU.subtract).then_inc(hid_lo, 1)

                nc.gpsimd.memset(sums[:, :], 1.0).then_inc(sums_set, 1)

                def step(t):
                    old, now, nxt, far = t - 1, t, t + 1, t + 2
                    if live(old):
                        hidden_low(old, G1 - 1)
                    if live(far):
                        wait(pool, padded, 1, far, 1)
                        nc.gpsimd.tensor_tensor(pair[:, :, :], xnT[:, :, 0:T + 2], xnT[:, :, 1:T + 3], ALU.add).then_inc(paired, 1)
                        wait(pool, paired, 1, far, 1)
                        wait(pool, fold_split, 1, far - 1, 1)
                        nc.gpsimd.tensor_tensor(fold[:, :, :], pair[:, :, 0:T], pair[:, :, 2:T + 2], ALU.add).then_inc(folded, 1)
                    if live(old):
                        wait(pool, x_again_in, 16, old, 16)
                        wait(pool, x1_done, 1, old - 1, 1)
                        nc.gpsimd.tensor_tensor(x_b2[:, :, :], x_again[:, :, :], ffn_b2[:, :].unsqueeze(1).to_broadcast([P, TT, D]), ALU.add).then_inc(x_kept, 1)
                    if live(nxt):
                        wait(pool, xT_hi, 1, nxt, 1)
                        nc.gpsimd.tensor_tensor(xT_l[:, :, :], xT[:, :, :], xT_h[:, :, :].bitcast(F32), ALU.subtract).then_inc(xT_lo, 1)
                    if live(now):
                        for g in range(G1 - 1):
                            hidden_low(now, g)
                steps(pool, step)

            @block.vector
            def _(dve):
                link = Links(dve, links)

                def split(hi, lo, src):
                    link(nc.vector.tensor_copy(hi, src))
                    return nc.vector.tensor_tensor(lo, src, hi.bitcast(F32), ALU.subtract)

                dve.wait_ge(sums_set, 1)

                def step(t):
                    old, now, nxt, far = t - 1, t, t + 1, t + 2
                    if live(now) or live(nxt) or live(far):
                        wait(dve, x_squared, 1, far, 1)
                        wait(dve, y_squared, 1, now, 1)
                        wait(dve, gf_squared, 1, nxt, 1)
                        nc.vector.tensor_scalar(sums[:, OF_G:], sums[:, OF_G:], NORM_EPS ** 2, None, ALU.max)
                        link(nc.vector.tensor_scalar(sums[:, 0:OF_G], sums[:, 0:OF_G], 1.0 / D, RMS_EPS, ALU.mult, ALU.add))
                        for k in range(RSQRT_OPS):
                            link(rsqrt_op(nc, k, sums[:, :], root[:, :], root_t[:, :]))
                    if live(far):
                        wait(dve, xn_T, 1, far - 1, 1)
                        for i in range(TT):
                            last = nc.vector.tensor_scalar(xn[:, i, :], x_t[:, i, :], root[:, OF_X + i:OF_X + i + 1], None, ALU.mult)
                        last.then_inc(x_scaled, 1)
                    if live(now):
                        wait(dve, h_T, 1, now - 1, 1)
                        for i in range(TT):
                            last = nc.vector.tensor_scalar(hn[:, i, :], y[:, i, :], root[:, OF_Y + i:OF_Y + i + 1], None, ALU.mult)
                        last.then_inc(hn_done, 1)
                    if live(nxt):
                        wait(dve, dotted, 1, nxt, 1)
                        link(nc.vector.tensor_tensor(dots[:, :], dots[:, :], root[:, OF_G:], ALU.mult))
                        link(nc.vector.tensor_scalar(dots[:, :], dots[:, :], trow_b[:, D:D + 1], 1.0, ALU.mult, ALU.add))
                        link(nc.vector.tensor_scalar(mix[:, :], dots[:, :], trow_b[:, D + 1:D + 2], None, ALU.mult))
                        link(nc.vector.tensor_scalar(keep[:, :], mix[:, :], -1.0, 1.0, ALU.mult, ALU.add))
                    if live(nxt):
                        wait(dve, bl_T, 1, nxt - 1, 1)
                        nc.vector.tensor_scalar(gfs[:, 0, :], gf[:, 0, :], keep[:, 0:1], None, ALU.mult)
                        link(nc.vector.tensor_scalar(gfs[:, 1, :], gf[:, 1, :], keep[:, 1:2], None, ALU.mult))
                        for i in range(TT):
                            last = nc.vector.scalar_tensor_tensor(blend[:, i, :], trow_b[:, 0:D], mix[:, i:i + 1], gfs[:, i, :], ALU.mult, ALU.add)
                        last.then_inc(blended, 1)
                    if live(far):
                        wait(dve, xnT_out, 1, far, 1)
                        nc.vector.tensor_copy(xnT[:, :, T:T + 3], xnT[:, :, T - 1:T].to_broadcast([P, KT, 3])).then_inc(padded, 1)
                    if live(nxt):
                        wait(dve, bl_hi, 1, nxt, 1)
                        wait(dve, mrg_done, 1, nxt - 1, 1)
                        nc.vector.tensor_tensor(bl_l[:, :, :].rearrange("p k t -> p (k t)"), bl_bank[:, :],
                                                bl_h[:, :, :].rearrange("p k t -> p (k t)").bitcast(F32), ALU.subtract).then_inc(bl_lo, 1)
                    if live(far):
                        wait(dve, folded, 1, far, 1)
                        wait(dve, pre_done, 1, far - 1, 1)
                        split(fold_h[:, :, :], fold_l[:, :, :], fold[:, :, :]).then_inc(fold_split, 1)
                    if live(now):
                        wait(dve, hT_out, 1, now, 1)
                        wait(dve, ffn1_done, G1, now - 1, G1)
                        split(h_h[:, :, :], h_l[:, :, :], hT[:, :, :]).then_inc(h_split, 1)
                    if live(old):
                        wait(dve, ffn2_done, TT, old, TT)
                        wait(dve, x_kept, 1, old, 1)
                        wait(dve, x1_out, 16, old - 1, 16)
                        nc.vector.tensor_tensor(x1[:, :, :], out_bank[:, :].rearrange("p (t d) -> p t d", t=TT), x_b2[:, :, :],
                                                ALU.add).then_inc(x1_done, 1)
                    if live(far):
                        wait(dve, pre_done, 1, far, 1)
                        wait(dve, blended, 1, far - 1, 1)
                        nc.vector.tensor_tensor(gf[:, :, :].rearrange("p t d -> p (t d)"), pre_bank[:, :],
                                                gate[:, :, :].rearrange("p t d -> p (t d)"), ALU.mult).then_inc(gf_done, 1)
                        wait(dve, gf_done, 1, far, 1)
                        wait(dve, row_in, 16, far, 16)
                        for i in range(TT):
                            last = nc.vector.tensor_tensor_reduce(out=junk[:, :], in0=gf[:, i, :], in1=trow_b[:, 0:D], scale=1.0,
                                                                  scalar=0.0, op0=ALU.mult, op1=ALU.add, accum_out=dots[:, i:i + 1])
                            last.then_inc(dotted, 1) if i == TT - 1 else link(last)
                    if live(nxt):
                        wait(dve, mrg_done, 1, nxt, 1)
                        wait(dve, hn_done, 1, nxt - 1, 1)
                        nc.vector.tensor_tensor(y[:, :, :], mrg_bank[:, :].rearrange("p (t d) -> p t d", t=TT),
                                                merge_b[:, :].unsqueeze(1).to_broadcast([P, TT, D]), ALU.add).then_inc(y_done, 1)
                steps(dve, step, link, LINKS_FIRST)


LINKS_FIRST = 20


TR_FILLS = [("proj", 0, 2), ("qk", 0, 4), ("qk", 1, 5), ("qk", 2, 6), ("qk", 3, 7), ("x2", 0, 8), ("h", 0, 9), ("gates", 0, 10),
            ("qk", 4, 11), ("qk", 5, 12), ("qk", 6, 13), ("qk", 7, 14)]
TR_LAG = {"h": 2, "proj": -1, "x2": -1, "gates": -1, "qk": 1}
TR_PER = {"h": 1, "proj": 1, "x2": 1, "gates": 1, "qk": 8}
CHUNKS = [(0, 0), (0, 1), (0, 2), (0, 3), (1, 0), (1, 1), (1, 2), (1, 3), (0, 4), (0, 5), (1, 4), (1, 5)]
CHUNK_SLOTS = [12, 13, 14, 15, 0, 1, 4, 5, 6, 7, 8, 9]
AHEAD = 4
SLOTS = H
SUM_SLOT, NORM_SLOT = (1, 9), (4, 11)
SPOTS = 6
LN_SLOT = 3
QKC = 4


def attention(nc, weights, banks, ident, x1_rows, hbias, cols, x2_rows, logit, out, sbuf, sems):
    landing, qk_raw, v_raw, o_raw, center, wgate, loaded = weights
    s = ExitStack()
    with s:
        wq_h, wq_l = (sbuf(s, f"wqkv_{p}", [P, KT, 3 * HW], F32R) for p in "hl")
        wo_h, wo_l = (sbuf(s, f"wout_{p}", [P, HW // P, D], F32R) for p in "hl")

        with ExitStack() as u:
            centered, hi_done, lo_done, q_scaled = sems(u, "centered att_hi att_lo q_scaled")
            flat = lambda t: t.rearrange("p k n -> p (k n)")
            with nc.Block() as block:
                @block.tensor
                def _(pe):
                    pe.wait_ge(loaded, 80)
                    for k in range(KT):
                        for m in range(2 * HW // P):
                            last = nc.tensor.matmul(banks[k * 4 + m // 4][:, m % 4 * P:(m % 4 + 1) * P],
                                                    qk_raw[:, m, k * P:(k + 1) * P], center[:, :], start=True, stop=True)
                            if m % 4 == 3:
                                last.then_inc(centered, 1)

                @block.scalar
                def _(act):
                    act.wait_ge(loaded, 80)
                    for k in range(KT):
                        nc.scalar.activation(wq_h[:, k, 2 * HW:], v_raw[:, k, :], ACT.Copy).then_inc(hi_done, 1)
                    nc.scalar.activation(flat(wo_h[:, :, :]), flat(o_raw), ACT.Copy).then_inc(hi_done, 1)
                    for f in range(8):
                        act.wait_ge(centered, f + 1)
                        nc.scalar.activation(wq_h[:, f // 4, f % 4 * 512:(f % 4 + 1) * 512], banks[f][:, :], ACT.Copy).then_inc(hi_done, 1)

                @block.gpsimd
                def _(pool):
                    for k in range(KT):
                        pool.wait_ge(hi_done, k + 1)
                        nc.gpsimd.tensor_tensor(wq_l[:, k, 2 * HW:], v_raw[:, k, :], wq_h[:, k, 2 * HW:].bitcast(F32), ALU.subtract).then_inc(lo_done, 1)

                @block.vector
                def _(dve):
                    nc.vector.tensor_scalar(cols[:, QN_G:QN_B + 1], cols[:, QN_G:QN_B + 1], -HD ** -0.5, None, ALU.mult).then_inc(q_scaled, 1)
                    dve.wait_ge(q_scaled, 1)
                    dve.wait_ge(hi_done, 3)
                    nc.vector.tensor_tensor(flat(wo_l[:, :, :]), flat(o_raw), flat(wo_h[:, :, :]).bitcast(F32), ALU.subtract).then_inc(lo_done, 1)
                    for f in range(8):
                        dve.wait_ge(hi_done, f + 4)
                        hi = wq_h[:, f // 4, f % 4 * 512:(f % 4 + 1) * 512]
                        nc.vector.tensor_tensor(wq_l[:, f // 4, f % 4 * 512:(f % 4 + 1) * 512], banks[f][:, :], hi.bitcast(F32), ALU.subtract).then_inc(lo_done, 1)

        stats = sbuf(s, "stats", [P, TT, 6])
        mean, var, rstd, vt = (sbuf(s, n, [P, TT]) for n in ("mean", "var", "rstd", "ln_t"))
        x1 = sbuf(s, "x1_t", [P, TT, D])
        aT = sbuf(s, "aT", [P, KT, T])
        a_h, a_l = (sbuf(s, f"a_{p}", [P, KT, T], F32R) for p in "hl")
        raw = sbuf(s, "raw_qk", [P, TT * QKC, 512])
        raw_sq = [sbuf(s, f"raw_sq{i}", [P, 512]) for i in range(2)]
        ssq = sbuf(s, "ssq", [P, TT, 2 * H])
        rq, rt = sbuf(s, "rq", [P, 2 * H]), sbuf(s, "rt", [P, 2 * H])
        qT, kT = ([landing[:, n + i, :].rearrange("p (h t) -> p h t", t=T) for i in range(2)] for n in (0, 2))
        v_h, v_l = ([sbuf(s, f"v_{p}{i}", [P, TT, H // 2, 3, HD], F32R) for i in range(2)] for p in "hl")
        shift = sbuf(s, "shift", [P, 2, TT])
        prob = [sbuf(s, f"prob{i}", [P, TT, T]) for i in range(2)]
        pT_h, pT_l = ([sbuf(s, f"pT_{p}{i}", [P, TT, T], F32R) for i in range(2)] for p in "hl")
        denom, share = sbuf(s, "denom", [P, 2, TT]), sbuf(s, "share_p", [P, 2, TT])
        o_h, o_l = (sbuf(s, f"o_{p}", [P, HW // P, T], F32R) for p in "hl")
        x2 = sbuf(s, "x2", [P, TT, D])
        proj = sbuf(s, "proj", [P, TT, D])
        x2T = proj
        tr, chunk_bank, score_bank, pT_bank, o_bank = banks[0], banks[1:3], banks[3:5], banks[5:7], banks[7]

        (zeros_set, x1_in, x1_again_in, normed_x, tr_h, tr_proj, tr_x2, tr_gates, tr_qk, out_h, out_proj, out_x2, out_gates, out_qk,
         a_hi, a_lo, chunk_done, chunk_out, v_lo, summed, rooted, normed, scored, lowest, exped, inverted, shared, pT_done, pT_hi, pT_lo,
         pv_done, o_hi, o_lo, x2_done, x2_stored, links) = sems(
            s, "zeros_set x1_in x1_again_in normed_x tr_h tr_proj tr_x2 tr_gates tr_qk out_h out_proj out_x2 out_gates out_qk "
               "a_hi a_lo chunk_done chunk_out v_lo summed rooted normed scored lowest exped inverted shared pT_done pT_hi pT_lo "
               "pv_done o_hi o_lo x2_done x2_stored att_links")
        drained = {"h": out_h, "proj": out_proj, "x2": out_x2, "gates": out_gates, "qk": out_qk}

        def tr_free(eng, t, name, j):
            at = [f[:2] for f in TR_FILLS].index((name, j))
            while True:
                at -= 1
                if at < 0:
                    at, t = at + len(TR_FILLS), t - 1
                    if isinstance(t, int) and t < -2:
                        return
                n, j, _ = TR_FILLS[at]
                b = t + TR_LAG[n]
                if live(b):
                    eng.wait_ge(drained[n], b * TR_PER[n] + j + 1)
                    return

        def steps(eng, step, link=None, per=0):
            for t in (-2, -1, 0, 1):
                step(t, t % 2)
            with eng.Fori(0, NB // 2 - 2) as i:
                if link:
                    link.enter(i, per)
                for odd in (0, 1):
                    step(i * 2 + 2 + odd, odd)
                if link:
                    link.leave(NB // 2 - 2)
            for t in range(NB - 2, NB + 1):
                step(t, t % 2)

        with nc.Block() as block:
            @block.sync
            def _(sp):
                def step(t, odd):
                    b = t + 2
                    if live(b):
                        wait(sp, tr_h, 1, b - 1, 1)
                        sp.dma_start(x1[:, :, :], x1_rows[bass.ds(b * T, T), :].rearrange("(t p) d -> p t d", p=P)).then_inc(x1_in, 16)
                    b = t - 1
                    if live(b):
                        wait(sp, tr_x2, 1, b - 1, 1)
                        sp.dma_start(x2[:, :, :], x1_rows[bass.ds(b * T, T), :].rearrange("(t p) d -> p t d", p=P)).then_inc(x1_again_in, 16)
                        wait(sp, x2_done, 1, b, 1)
                        for dst in (out, x2_rows):
                            sp.dma_start(dst[bass.ds(b * T, T), :].rearrange("(t p) d -> p t d", p=P), x2[:, :, :]).then_inc(x2_stored, 16)
                steps(sp, step)
                sp.wait_ge(x2_stored, 32 * NB)

            @block.tensor
            def _(pe):
                def step(t, odd):
                    for i in range(SLOTS):
                        if live(t):
                            hp, r = i // 2, slice(i % 2 * HD, (i % 2 + 1) * HD)
                            if i == 0:
                                wait(pe, out_qk, 8, t, 8)
                            wait(pe, exped, H, t, i - 1)
                            for n in range(TT):
                                last = nc.tensor.matmul(score_bank[i % 2][:, n * T:(n + 1) * T], qT[odd][r, hp, n * P:(n + 1) * P],
                                                        kT[odd][r, hp, :], start=True, stop=True)
                            last.then_inc(scored, 1)
                        b, j = chunk_at(t, i)
                        if j is not None and live(b):
                            n, c = CHUNKS[j]
                            if j == 0:
                                wait(pe, a_hi, 1, b, 1)
                                wait(pe, a_lo, 1, b, 1)
                            if 2 <= j < 2 + TT * QKC:
                                wait(pe, chunk_out, 12, b, j - 1)
                            else:
                                wait(pe, v_lo, 4, b, j - 1 if j < 2 else j - TT * QKC - 1)
                            product(nc, chunk_bank[j % 2][:, :],
                                    lambda k: (a_h[:, k, n * P:(n + 1) * P], a_l[:, k, n * P:(n + 1) * P]),
                                    lambda k: (wq_h[:, k, c * 512:(c + 1) * 512], wq_l[:, k, c * 512:(c + 1) * 512]),
                                    range(KT)).then_inc(chunk_done, 1)
                        b, h, _ = head_at(t, i, 1, odd)
                        if live(b):
                            wait(pe, shared, H, b, h + 1)
                            wait(pe, pT_lo, H, b, h - 1)
                            for m in range(TT):
                                for n in range(TT):
                                    last = nc.tensor.transpose(pT_bank[h % 2][:, m * T + n * P:m * T + (n + 1) * P], prob[h % 2][:, n, m * P:(m + 1) * P], ident[:, :])
                            last.then_inc(pT_done, 1)
                        b, h, its = head_at(t, i, 2, odd)
                        if live(b):
                            wait(pe, pT_lo, H, b, h + 1)
                            q = h // 2
                            if h == 0:
                                wait(pe, v_lo, 4, b, 4)
                                pe.wait_ge(zeros_set, 1)
                            if h % 2 == 0:
                                wait(pe, o_lo, H // 2, b, q)
                            x = 0
                            for m in range(TT):
                                vh, vl = (v[its][:, m, q, h % 2:h % 2 + 2, :].rearrange("p a d -> p (a d)") for v in (v_h, v_l))
                                ph, pl = (v[h % 2][:, m, :] for v in (pT_h, pT_l))
                                for l, r in ((vh, ph), (vh, pl), (vl, ph)):
                                    last = nc.tensor.matmul(o_bank[:, 0:T], l, r, start=(h % 2 == 0 and x == 0), stop=(h % 2 == 1 and x == 3 * TT - 1))
                                    x += 1
                            last.then_inc(pv_done, 1)
                        for name, j, slot in TR_FILLS:
                            b = t + TR_LAG[name]
                            if not live(b):
                                continue
                            if name == "proj" and slot <= i < slot + TT:
                                n = i - slot
                                if n == 0:
                                    wait(pe, o_lo, H // 2, b, H // 2)
                                    tr_free(pe, t, name, j)
                                last = product(nc, tr[:, n * D:(n + 1) * D],
                                               lambda k: (o_h[:, k, n * P:(n + 1) * P], o_l[:, k, n * P:(n + 1) * P]),
                                               lambda k: (wo_h[:, k, :], wo_l[:, k, :]), range(HW // P))
                                if n == TT - 1:
                                    last.then_inc(tr_proj, 1)
                            if slot != i:
                                continue
                            if name == "h":
                                wait(pe, normed_x, 1, b, 1)
                                tr_free(pe, t, name, j)
                                for k in range(KT):
                                    for n in range(TT):
                                        last = nc.tensor.transpose(tr[:, k * T + n * P:k * T + (n + 1) * P], x1[:, n, k * P:(k + 1) * P], ident[:, :])
                                last.then_inc(tr_h, 1)
                            if name == "qk":
                                wait(pe, normed, 8, b, j + 1)
                                tr_free(pe, t, name, j)
                                for m in range(4):
                                    last = nc.tensor.transpose(tr[:, m * P:(m + 1) * P], raw[:, j, m * P:(m + 1) * P], ident[:, :])
                                last.then_inc(tr_qk, 1)
                            if name == "x2":
                                wait(pe, x2_done, 1, b, 1)
                                wait(pe, x2_stored, 32, b, 32)
                                tr_free(pe, t, name, j)
                                for k in range(KT):
                                    for n in range(TT):
                                        last = nc.tensor.transpose(tr[:, k * T + n * P:k * T + (n + 1) * P], x2[:, n, k * P:(k + 1) * P], ident[:, :])
                                last.then_inc(tr_x2, 1)
                            if name == "gates":
                                wait(pe, out_x2, 1, b, 1)
                                tr_free(pe, t, name, j)
                                for n in range(TT):
                                    for k in range(KT):
                                        last = nc.tensor.matmul(tr[:, n * E:(n + 1) * E], x2T[:, k, n * P:(n + 1) * P], wgate[:, k, :],
                                                                start=(k == 0), stop=(k == KT - 1))
                                last.then_inc(tr_gates, 1)
                steps(pe, step)

            @block.scalar
            def _(act):
                def step(t, odd):
                    for i in range(SLOTS):
                        b, h, _ = head_at(t, i, 3, odd)
                        if h % 2 == 1 and live(b):
                            wait(act, pv_done, H, b, h + 1)
                            wait(act, tr_proj, 1, b - 1, 1)
                            nc.scalar.activation(o_h[:, h // 2, :], o_bank[:, 0:T], ACT.Copy).then_inc(o_hi, 1)
                        for name, j, slot in TR_FILLS:
                            b = t + TR_LAG[name]
                            if i != slot + (TT if name == "proj" else 1) or not live(b):
                                continue
                            if name == "h":
                                wait(act, tr_h, 1, b, 1)
                                wait(act, a_lo, 1, b - 1, 1)
                                for k in range(KT):
                                    last = nc.scalar.activation(aT[:, k, :], tr[:, k * T:(k + 1) * T], ACT.Identity,
                                                                bias=hbias[:, k, bass.ds(b, 1)], scale=cols[:, LN1_G + k:LN1_G + k + 1])
                                last.then_inc(out_h, 1)
                            if name == "qk":
                                wait(act, tr_qk, 8, b, j + 1)
                                dst, g = (qT, QN_G) if j % 4 < 2 else (kT, KN_G)
                                nc.scalar.activation(dst[1 - odd][:, j % 2 * 4:j % 2 * 4 + 4, j // 4 * P:(j // 4 + 1) * P],
                                                     tr[:, :].rearrange("p (m n) -> p m n", m=4), ACT.Identity,
                                                     bias=cols[:, g + 1:g + 2], scale=cols[:, g:g + 1]).then_inc(out_qk, 1)
                            if name == "proj":
                                wait(act, tr_proj, 1, b, 1)
                                wait(act, tr_gates, 1, b - 1, 1)
                                nc.scalar.activation(proj[:, :, :].rearrange("p k n -> p (k n)"), tr[:, :], ACT.Copy).then_inc(out_proj, 1)
                            if name == "x2":
                                wait(act, tr_x2, 1, b, 1)
                                nc.scalar.activation(x2T[:, :, :].rearrange("p k n -> p (k n)"), tr[:, :], ACT.Copy).then_inc(out_x2, 1)
                            if name == "gates":
                                wait(act, tr_gates, 1, b, 1)
                                nc.scalar.activation(logit[:, bass.ds(b * TT, TT), :], tr[:, 0:TT * E].rearrange("p (n e) -> p n e", n=TT), ACT.Copy).then_inc(out_gates, 1)
                        if live(t):
                            wait(act, lowest, H, t, i + 1)
                            wait(act, pT_done, H, t, i - 1)
                            for n in range(TT):
                                last = nc.scalar.activation(prob[i % 2][:, n, :], score_bank[i % 2][:, n * T:(n + 1) * T], ACT.Exp,
                                                            bias=shift[:, i % 2, n:n + 1], scale=-1.0,
                                                            accum_out=denom[:, i % 2, n:n + 1])
                            last.then_inc(exped, 1)
                        b, j = chunk_at(t, i)
                        if j is not None and live(b):
                            n, c = CHUNKS[j]
                            wait(act, chunk_done, 12, b, j + 1)
                            if c < QKC:
                                e = n * QKC + c
                                wait(act, tr_qk, 8, b - 1, e + 1)
                                nc.scalar.activation(raw[:, e, :], chunk_bank[j % 2][:, :], ACT.Copy)
                                wait(act, summed, 8, b, e - 1)
                                nc.scalar.activation(raw_sq[e % 2][:, :], chunk_bank[j % 2][:, :], ACT.Square).then_inc(chunk_out, 1)
                            else:
                                wait(act, pv_done, H, b - 2, H)
                                nc.scalar.activation(v_h[1 - odd][:, n, (c - QKC) * 4:(c - QKC + 1) * 4, 0:3:2, :],
                                                     chunk_bank[j % 2][:, :].rearrange("p (q h d) -> p q h d", q=4, h=2), ACT.Copy).then_inc(chunk_out, 1)
                        b, h, _ = head_at(t, i, 1, odd)
                        if live(b):
                            wait(act, pT_done, H, b, h + 1)
                            wait(act, pv_done, H, b, h - 1)
                            nc.scalar.activation(pT_h[h % 2][:, :, :].rearrange("p m n -> p (m n)"), pT_bank[h % 2][:, :], ACT.Copy).then_inc(pT_hi, 1)
                steps(act, step)

            @block.gpsimd
            def _(pool):
                for v in v_h + v_l:
                    last = nc.gpsimd.memset(v[:, :, :, 1, :].bitcast(F32), 0.0)
                last.then_inc(zeros_set, 1)

                def step(t, odd):
                    far, new, old = t + 2, t + 1, t - 1
                    for i in range(SLOTS):
                        for n in range(TT):
                            c = i - NORM_SLOT[n]
                            if live(new) and 0 <= c < QKC:
                                if c == 0:
                                    wait(pool, rooted, TT, new, n + 1)
                                nc.gpsimd.tensor_tensor(raw[:, n * QKC + c, :].rearrange("p (h d) -> p h d", h=8), raw[:, n * QKC + c, :].rearrange("p (h d) -> p h d", h=8),
                                                        rq[:, c * 8:(c + 1) * 8].unsqueeze(2).to_broadcast([P, 8, HD]), ALU.mult).then_inc(normed, 1)
                        if live(old) and i == 5:
                            wait(pool, out_proj, 1, old, 1)
                            wait(pool, x1_again_in, 16, old, 16)
                            nc.gpsimd.tensor_tensor(x2[:, :, :], proj[:, :, :], x2[:, :, :], ALU.add).then_inc(x2_done, 1)
                        if live(far) and i == 11:
                            wait(pool, a_hi, 1, far, 1)
                            wait(pool, chunk_done, 12, far - 1, 12)
                            nc.gpsimd.tensor_tensor(a_l[:, :, :], aT[:, :, :], a_h[:, :, :].bitcast(F32), ALU.subtract).then_inc(a_lo, 1)
                        if live(t):
                            wait(pool, inverted, H, t, i + 1)
                            nc.gpsimd.tensor_tensor(prob[i % 2][:, :, :], prob[i % 2][:, :, :],
                                                    share[:, i % 2, :].unsqueeze(2).to_broadcast([P, TT, T]), ALU.mult).then_inc(shared, 1)
                steps(pool, step)

            @block.vector
            def _(dve):
                link = Links(dve, links)

                def chains(t, i, spot):
                    new, far = t + 1, t + 2
                    for n in range(TT):
                        k = (i - SUM_SLOT[n]) * SPOTS + spot
                        if live(new) and 0 <= k <= RSQRT_OPS:
                            if k == 0:
                                wait(dve, summed, 8, new, (n + 1) * QKC)
                                link.note(nc.vector.tensor_scalar(ssq[:, n, :], ssq[:, n, :], 1.0 / HD, LN_EPS, ALU.mult, ALU.add))
                            else:
                                wait(dve, normed, 8, new, n * QKC)
                                link.settle()
                                ins = rsqrt_op(nc, k - 1, ssq[:, n, :], rq[:, :], rt[:, :])
                                ins.then_inc(rooted, 1) if k == RSQRT_OPS else link.note(ins)
                    k = (i - LN_SLOT) * SPOTS + spot
                    if live(far) and 0 <= k < TT:
                        wait(dve, x1_in, 16, far, 16)
                        link.note(nc.vector.bn_stats(stats[:, k, :], x1[:, k, :]))
                    k -= TT
                    if live(far) and 0 <= k < MOMENTS_OPS:
                        link.settle()
                        link.note(moments_op(nc, k, stats, mean[:, :], var[:, :], vt[:, :]))
                    k -= MOMENTS_OPS
                    if live(far) and 0 <= k < RSQRT_OPS:
                        link.settle()
                        link.note(rsqrt_op(nc, k, var[:, :], rstd[:, :], vt[:, :]))
                    k -= RSQRT_OPS
                    if live(far) and 0 <= k < TT:
                        link.settle()
                        ins = nc.vector.tensor_scalar(x1[:, k, :], x1[:, k, :], mean[:, k:k + 1], rstd[:, k:k + 1], ALU.subtract, ALU.mult)
                        ins.then_inc(normed_x, 1) if k == TT - 1 else link.note(ins)

                def step(t, odd):
                    far, new = t + 2, t + 1
                    for i in range(SLOTS):
                        chains(t, i, 0)
                        b, h, _ = head_at(t, i, 2, odd)
                        if live(b):
                            wait(dve, pT_hi, H, b, h + 1)
                            wait(dve, pv_done, H, b, h - 1)
                            nc.vector.tensor_tensor(pT_l[h % 2][:, :, :].rearrange("p m n -> p (m n)"), pT_bank[h % 2][:, :],
                                                    pT_h[h % 2][:, :, :].rearrange("p m n -> p (m n)").bitcast(F32), ALU.subtract).then_inc(pT_lo, 1)
                        b, h, _ = head_at(t, i, 3, odd)
                        if h % 2 == 1 and live(b):
                            wait(dve, o_hi, H // 2, b, h // 2 + 1)
                            nc.vector.tensor_tensor(o_l[:, h // 2, :], o_bank[:, 0:T], o_h[:, h // 2, :].bitcast(F32), ALU.subtract).then_inc(o_lo, 1)
                        chains(t, i, 1)
                        if live(t):
                            wait(dve, scored, H, t, i + 1)
                            wait(dve, exped, H, t, i - 1)
                            nc.vector.tensor_reduce(shift[:, i % 2, :], score_bank[i % 2][:, :].rearrange("p (n m) -> p n m", n=TT), AX, ALU.min).then_inc(lowest, 1)
                        chains(t, i, 2)
                        chains(t, i, 3)
                        b, j = chunk_at(t, i - 1)
                        if j is not None and live(b):
                            n, c = CHUNKS[j]
                            wait(dve, chunk_out, 12, b, j + 1)
                            if c < QKC:
                                nc.vector.tensor_reduce(ssq[:, n, c * 8:(c + 1) * 8], raw_sq[c % 2][:, :].rearrange("p (h d) -> p h d", h=8), AX, ALU.add).then_inc(summed, 1)
                            else:
                                nc.vector.tensor_tensor(v_l[1 - odd][:, n, (c - QKC) * 4:(c - QKC + 1) * 4, 0:3:2, :],
                                                        chunk_bank[j % 2][:, :].rearrange("p (q h d) -> p q h d", q=4, h=2),
                                                        v_h[1 - odd][:, n, (c - QKC) * 4:(c - QKC + 1) * 4, 0:3:2, :].bitcast(F32), ALU.subtract).then_inc(v_lo, 1)
                        chains(t, i, 4)
                        if live(far) and i == 10:
                            wait(dve, out_h, 1, far, 1)
                            wait(dve, chunk_done, 12, far - 1, 12)
                            nc.vector.tensor_copy(a_h[:, :, :], aT[:, :, :]).then_inc(a_hi, 1)
                        if live(t):
                            wait(dve, exped, H, t, i + 1)
                            wait(dve, shared, H, t, i - 1)
                            nc.vector.reciprocal(share[:, i % 2, :], denom[:, i % 2, :]).then_inc(inverted, 1)
                        chains(t, i, 5)
                steps(dve, step, link, LINKS_ATTENTION)


LINKS_ATTENTION = 86


def experts(nc, a, banks, ident, cols, x2_rows, logit, out, sbuf, sems):
    s = ExitStack()
    with s:
        steps32, steps16 = sbuf(s, "steps32", [P, 32]), sbuf(s, "steps16", [P, 16])
        quarter, token = sbuf(s, "quarter", [P, 4]), sbuf(s, "token", [P, TILES])
        spread = sbuf(s, "spread", [32, P], F32R)
        gates = sbuf(s, "gates", [P, TILES, E])
        gate_h, gate_l = (sbuf(s, f"gate_{p}", [P, TILES, E], F32R) for p in "hl")
        low, high = sbuf(s, "slot_low", [P, TILES, E]), sbuf(s, "slot_high", [P, TILES, E])

        b1 = sbuf(s, "b1", [P, E * G2])
        w1, w2 = sbuf(s, "ew1", [P, KT, DD]), sbuf(s, "ew2", [P, G2, D])
        w1_h, w1_l = (sbuf(s, f"ew1_{p}", [P, KT, DD], F32R) for p in "hl")
        w2_h, w2_l = (sbuf(s, f"ew2_{p}", [P, G2, D], F32R) for p in "hl")
        b2 = sbuf(s, "eb2", [P, E, D])
        b1_in, w1_in, w2_in, b2_in, w1_hi, w1_lo, w2_hi, w2_lo = sems(s, "b1_in w1_in w2_in b2_in w1_hi w1_lo w2_hi w2_lo")

        def load_w1(sp, at):
            sp.dma_start(w1[:, :, :], a["fc1s"][bass.ds(at, D), :].rearrange("(k p) n -> p k n", p=P)).then_inc(w1_in, 16)

        def load_w2(sp, at):
            sp.dma_start(w2[:, :, :], a["fc2s"][bass.ds(at, DD), :].rearrange("(k p) n -> p k n", p=P)).then_inc(w2_in, 16)

        def high_part(w, w_h):
            return nc.scalar.activation(w_h[:, :, :], w[:, :, :], ACT.Copy)

        def low_part(w, w_h, w_l):
            return nc.gpsimd.tensor_tensor(w_l[:, :, :], w[:, :, :], w_h[:, :, :].bitcast(F32), ALU.subtract)

        with ExitStack() as u:
            peak, denom = sbuf(u, "peak", [P, TILES]), sbuf(u, "gate_sum", [P, TILES])
            tables = sbuf(u, "tables", [P, 4 * P])
            earlier, ones = (sbuf(u, n, [P, P], mybir.dt.bfloat16) for n in ("earlier", "ones_b"))
            by_expert = sbuf(u, "by_expert", [P, 2 * P])
            junk = sbuf(u, "count_junk", [P, 3, 2 * P], mybir.dt.bfloat16)
            count, passed = sbuf(u, "count", [P, 3]), sbuf(u, "passed", [P, 3])
            units, trial = sbuf(u, "units", [P, 3], I32), sbuf(u, "trial", [P, 3], I32)
            digit, unit = sbuf(u, "digit", [P, 1]), sbuf(u, "unit", [P, 1])
            prefix, placed_digit = sbuf(u, "prefix", [P, 1], I32), sbuf(u, "placed_digit", [P, 1], I32)
            above, tied = sbuf(u, "above", [P, 2 * P]), sbuf(u, "tied", [P, 2 * P])
            above_b, tied_b, chosen_b = (sbuf(u, n, [P, TILES, E], mybir.dt.bfloat16) for n in ("above_b", "tied_b", "chosen_b"))
            above_s = sbuf(u, "above_s", [P, E])
            above_n = sbuf(u, "above_n", [P, 1, E], mybir.dt.bfloat16)
            chosen, slot = sbuf(u, "chosen", [P, TILES, E]), sbuf(u, "slot", [P, TILES, E])
            slot_i, part_i = sbuf(u, "slot_i", [P, TILES, E], I32), sbuf(u, "part_i", [P, TILES, E], I32)
            flat = lambda t: t[:, :, :].rearrange("p t e -> p (t e)")
            (loaded, centred, exped, gated, tr_gates, counted, totalled, summed, masked, tr_masks, masks_out, ranked, chose,
             placed, links) = sems(u, "rt_loaded rt_centred rt_exped rt_gated rt_tr_gates counted totalled rt_summed masked "
                                   "tr_masks masks_out ranked chose placed route_links")
            DIGITS, TURN = 15, 3
            with nc.Block() as block:
                @block.sync
                def _(sp):
                    for t, src in ((tables[:, :], a["tables"]), (steps32[:, :], a["counts"][:, 0:32]), (steps16[:, :], a["counts"][:, 0:16]),
                                   (quarter[:, :], a["counts"][:, 32:36]), (token[:, :], a["counts"][:, 36:36 + TILES])):
                        sp.dma_start(t, src).then_inc(loaded, 16)
                    load_w1(sp, 0)
                    load_w2(sp, 0)
                    sp.dma_start(b1[:, :], a["b1s"]).then_inc(b1_in, 16)
                    sp.dma_start(b2[:, :, :], a["b2s"].unsqueeze(0).to_broadcast([P, E, D])).then_inc(b2_in, 16)

                @block.scalar
                def _(act):
                    act.wait_ge(centred, 1)
                    nc.scalar.activation(gates[:, :, :], gates[:, :, :], ACT.Exp).then_inc(exped, 1)
                    act.wait_ge(w1_in, 16)
                    high_part(w1, w1_h).then_inc(w1_hi, 1)
                    act.wait_ge(w2_in, 16)
                    high_part(w2, w2_h).then_inc(w2_hi, 1)

                @block.gpsimd
                def _(pool):
                    pool.wait_ge(w1_hi, 1)
                    low_part(w1, w1_h, w1_l).then_inc(w1_lo, 1)
                    pool.wait_ge(w2_hi, 1)
                    low_part(w2, w2_h, w2_l).then_inc(w2_lo, 1)

                @block.tensor
                def _(pe):
                    pe.wait_ge(gated, 1)
                    for i in range(2):
                        last = nc.tensor.transpose(banks[0][:, i * P:(i + 1) * P], flat(gates)[:, i * P:(i + 1) * P], ident[:, :])
                    last.then_inc(tr_gates, 1)
                    with pe.Fori(0, DIGITS // TURN) as i:
                        for k in range(TURN):
                            pe.wait_ge(counted, i * TURN + k + 1)
                            nc.tensor.matmul(banks[1][:, 0:3], tables[:, P:2 * P], count[:, :], start=True, stop=True).then_inc(totalled, 1)
                    pe.wait_ge(masked, 1)
                    for n, m in enumerate((above, tied)):
                        for i in range(2):
                            last = nc.tensor.transpose(banks[2 + n][:, i * P:(i + 1) * P], m[:, i * P:(i + 1) * P], ident[:, :])
                    last.then_inc(tr_masks, 1)
                    def earlier_count(bank, mask, first):
                        nc.tensor.matmul(bank[:, 0:TILES * E], earlier[:, :], flat(mask), start=True, stop=False)
                        for i in range(TILES - 1):
                            last = nc.tensor.matmul(bank[:, (i + 1) * E:TILES * E].rearrange("p (t e) -> p t e", e=E), ones[:, :],
                                                    mask[:, i:i + 1, :].to_broadcast([P, TILES - 1 - i, E]), start=False,
                                                    stop=(not first and i == TILES - 2))
                        return last
                    pe.wait_ge(masks_out, 1)
                    earlier_count(banks[4], tied_b, True)
                    pe.wait_ge(summed, 1)
                    nc.tensor.matmul(banks[4][:, 0:TILES * E].rearrange("p (t e) -> p t e", e=E), ones[:, :],
                                     above_n[:, :, :].to_broadcast([P, TILES, E]), start=False, stop=True).then_inc(ranked, 1)
                    pe.wait_ge(chose, 1)
                    earlier_count(banks[5], chosen_b, False).then_inc(placed, 1)

                @block.vector
                def _(dve):
                    link = Links(dve, links)
                    vec = nc.vector
                    wide = lambda t: t[:, :].unsqueeze(2).to_broadcast([P, TILES, E])
                    link(vec.reduce_max(peak[:, :], logit[:, :, :], AX))
                    vec.tensor_tensor(gates[:, :, :], logit[:, :, :], wide(peak), ALU.subtract).then_inc(centred, 1)
                    dve.wait_ge(exped, 1)
                    link(vec.tensor_reduce(denom[:, :], gates[:, :, :], AX, ALU.add))
                    link(vec.reciprocal(denom[:, :], denom[:, :]))
                    vec.tensor_tensor(gates[:, :, :], gates[:, :, :], wide(denom), ALU.mult).then_inc(gated, 1)
                    dve.wait_ge(gated, 1)
                    link(vec.tensor_copy(gate_h[:, :, :], gates[:, :, :]))
                    vec.tensor_tensor(gate_l[:, :, :], gates[:, :, :], gate_h[:, :, :].bitcast(F32), ALU.subtract)
                    dve.wait_ge(loaded, 80)
                    vec.tensor_copy(earlier[:, :], tables[:, 0:P])
                    vec.memset(ones[:, :], 1.0)
                    vec.tensor_copy(spread[:, :], tables[0:32, 2 * P:3 * P])
                    vec.memset(prefix[:, :], 0)
                    for k in range(3):
                        vec.memset(units[:, k:k + 1], (k + 1) << (2 * DIGITS - 2))
                    link(vec.memset(unit[:, :], float(1 << (2 * DIGITS - 2))))
                    dve.wait_ge(tr_gates, 1)
                    link(vec.tensor_copy(by_expert[:, :], banks[0][:, 0:2 * P]))
                    link(vec.tensor_copy(trial[:, :], units[:, :]))
                    with dve.Fori(0, DIGITS // TURN) as i:
                        link.enter(i, 6 * TURN)
                        for n in range(TURN):
                            if n:
                                link.settle()
                            for k in range(3):
                                last = vec.tensor_scalar(junk[:, k, :], by_expert[:, :], trial[:, k:k + 1].bitcast(F32), None, ALU.is_ge, ALU.add,
                                                         accum_out=count[:, k:k + 1])
                            last.then_inc(counted, 1)
                            link.note(vec.tensor_scalar(units[:, :], units[:, :], 2, None, ALU.logical_shift_right))
                            dve.wait_ge(totalled, i * TURN + n + 1)
                            link.note(vec.tensor_scalar(passed[:, :], banks[1][:, 0:3], float(CAP), None, ALU.is_ge, ALU.add, accum_out=digit[:, :]))
                            link.settle()
                            link.note(vec.tensor_scalar(placed_digit[:, :], digit[:, :], unit[:, 0:1], None, ALU.mult))
                            link.note(vec.tensor_scalar(unit[:, :], unit[:, :], 0.25, None, ALU.mult))
                            link.settle()
                            link.note(vec.tensor_tensor(prefix[:, :], prefix[:, :], placed_digit[:, :], ALU.bitwise_or))
                            link.settle()
                            link.note(vec.tensor_tensor(trial[:, :], units[:, :], prefix[:, :].to_broadcast([P, 3]), ALU.bitwise_or))
                        link.settle()
                        link.leave(DIGITS // TURN)
                    least = prefix[:, :].bitcast(F32)
                    link(vec.tensor_scalar(above[:, :], by_expert[:, :], least, None, ALU.is_gt))
                    vec.tensor_scalar(tied[:, :], by_expert[:, :], least, None, ALU.is_equal).then_inc(masked, 1)
                    dve.wait_ge(tr_masks, 1)
                    link(vec.tensor_copy(flat(above_b), banks[2][:, 0:2 * P]))
                    vec.tensor_copy(flat(tied_b), banks[3][:, 0:2 * P]).then_inc(masks_out, 1)
                    link(vec.tensor_reduce(above_s[:, :], above_b[:, :, :].rearrange("p t e -> p e t"), AX, ALU.add))
                    vec.tensor_copy(above_n[:, 0, :], above_s[:, :]).then_inc(summed, 1)
                    dve.wait_ge(ranked, 1)
                    dve.wait_ge(masks_out, 1)
                    link(vec.scalar_tensor_tensor(flat(chosen), banks[4][:, 0:TILES * E], float(CAP), flat(tied_b), ALU.is_lt, ALU.mult))
                    link(vec.tensor_tensor(flat(chosen), flat(chosen), flat(above_b), ALU.add))
                    vec.tensor_copy(flat(chosen_b), flat(chosen)).then_inc(chose, 1)
                    dve.wait_ge(placed, 1)
                    link(vec.scalar_tensor_tensor(flat(slot), banks[5][:, 0:TILES * E], 1.0, flat(chosen), ALU.add, ALU.mult))
                    link(vec.tensor_scalar(flat(slot_i), flat(slot), -1.0, None, ALU.add))
                    link(vec.tensor_scalar(flat(part_i), flat(slot_i), 31, None, ALU.bitwise_and))
                    link(vec.tensor_copy(flat(low), flat(part_i)))
                    link(vec.tensor_scalar(flat(part_i), flat(slot_i), 5, None, ALU.arith_shift_right))
                    link(vec.tensor_copy(flat(high), flat(part_i)))

        in_row = sbuf(s, "in_row", [P, TILES, 32], F32R)
        in_col = sbuf(s, "in_col", [P, TILES, 16])
        record = sbuf(s, "record", [P, TILES, 3, 16], F32R)
        rec32 = sbuf(s, "rec32", [32, 48], F32R)
        picked = sbuf(s, "picked", [P, 3 * CC, 4])
        fields = sbuf(s, "fields", [P, 3, CC])
        index = [sbuf(s, f"index{i}", [P, CC], U32) for i in range(2)]
        share = [sbuf(s, f"share{i}", [P, CC]) for i in range(2)]
        next_index, next_share = sbuf(s, "next_index", [P, CC], U32), sbuf(s, "next_share", [P, CC])
        gx = sbuf(s, "gx", [P, CC, D])
        stats = sbuf(s, "e_stats", [P, CC, 6])
        mean, var, rstd, vt = (sbuf(s, n, [P, CC]) for n in ("e_mean", "e_var", "e_rstd", "e_t"))
        gn = sbuf(s, "gn", [P, CC, D])
        gT = sbuf(s, "gT", [P, KT, CAP])
        g_h, g_l = (sbuf(s, f"g_{p}", [P, KT, CAP], F32R) for p in "hl")
        hid = sbuf(s, "ehid", [P, G2, CAP])
        hid_h, hid_l = (sbuf(s, f"ehid_{p}", [P, G2, CAP], F32R) for p in "hl")
        y, yw = sbuf(s, "ey", [P, CC, D]), sbuf(s, "eyw", [P, CC, D])
        idle = sbuf(s, "idle", [P, 2])
        rec_bank, tr_banks, fc1_bank, fc2_bank = banks[0], banks[1:3], banks[3:5], banks[5:7]
        (held, built, rec_done, rec_out, spread_done, indexed, gathered,
         gn_done, tr_done, gT_out, g_split, fc1_done, gelu_done, hid_hi, hid_lo, fc2_done, y_done, scattered, links) = sems(
            s, "held built rec_done rec_out spread_done indexed gathered "
               "gn_done tr_done gT_out g_split e_fc1_done e_gelu_done e_hid_hi e_hid_lo e_fc2_done y_out scattered expert_links")

        def there(e):
            return not isinstance(e, int) or 0 <= e < E

        def first(e):
            return isinstance(e, int) and e == 0

        def wait_e(eng, sem, per, e, n):
            if n <= 0:
                e, n = e - 1, n + per
            if there(e):
                eng.wait_ge(sem, e * per + n)

        def steps(eng, step, link=None, per=0):
            for t in range(-3, 1):
                step(t, t % 2)
            with eng.Fori(0, (E - 3) // 2) as i:
                if link:
                    link.enter(i, per)
                for odd in (1, 0):
                    step(i * 2 + (2 - odd), odd)
                if link:
                    link.leave((E - 3) // 2)
            for t in range(1 + (E - 3) // 2 * 2, E):
                step(t, t % 2)

        with nc.Block() as block:
            @block.sync
            def _(sp):
                def step(t, odd):
                    e = t + 1
                    if there(e) and not first(e):
                        at1, at2 = e * D, e * DD
                        if not isinstance(e, int):
                            e, at1, at2 = sp.snap(e), sp.snap(at1), sp.snap(at2)
                        wait_e(sp, w1_lo, 1, e - 1, 1)
                        load_w1(sp, at1)
                        wait_e(sp, w2_lo, 1, e - 1, 1)
                        load_w2(sp, at2)
                steps(sp, step)

            @block.tensor
            def _(pe):
                def fc1(t, m):
                    if m == 0:
                        wait_e(pe, w1_lo, 1, t, 1)
                        wait_e(pe, g_split, 1, t, 1)
                    wait_e(pe, gelu_done, G2, t, m - 1)
                    product(nc, fc1_bank[m % 2][:, :], lambda k: (w1_h[:, k, m * P:(m + 1) * P], w1_l[:, k, m * P:(m + 1) * P]),
                            lambda k: (g_h[:, k, :], g_l[:, k, :]), range(KT)).then_inc(fc1_done, 1)

                def fc2(t, c):
                    def hidden(k):
                        if c == 0:
                            wait_e(pe, hid_lo, G2, t, k + 1)
                        return hid_h[:, k, c * P:(c + 1) * P], hid_l[:, k, c * P:(c + 1) * P]
                    if c == 0:
                        wait_e(pe, w2_lo, 1, t, 1)
                    if c % 2 == 0:
                        wait_e(pe, y_done, CC, t - 1, c + 2)
                    product(nc, fc2_bank[c // 2][:, c % 2 * D:(c % 2 + 1) * D], hidden,
                            lambda k: (w2_h[:, k, :], w2_l[:, k, :]), range(G2)).then_inc(fc2_done, 1)

                def step(t, odd):
                    new, later = t + 1, t + 2
                    if there(t):
                        for m in range(G2):
                            fc1(t, m)
                    if there(later):
                        wait_e(pe, built, 1, later, 1)
                        wait_e(pe, indexed, 1, later - 1, 1)
                        for i in range(TILES):
                            last = nc.tensor.matmul(rec_bank[0:32, 0:48], in_row[:, i, :], record[:, i, :, :].rearrange("p c n -> p (c n)"),
                                                    start=(i == 0), stop=(i == TILES - 1))
                        last.then_inc(rec_done, 1)
                    if there(t):
                        fc2(t, 0)
                    if there(later):
                        wait_e(pe, rec_out, 1, later, 1)
                        nc.tensor.matmul(rec_bank[:, 64:112], spread[:, :], rec32[:, :], start=True, stop=True).then_inc(spread_done, 1)
                    if there(new):
                        wait_e(pe, gn_done, 1, new, 1)
                        wait_e(pe, gT_out, 1, new - 1, 1)
                        for k in range(KT):
                            for c in range(CC):
                                last = nc.tensor.transpose(tr_banks[k][:, c * P:(c + 1) * P], gn[:, c, k * P:(k + 1) * P], ident[:, :])
                        last.then_inc(tr_done, 1)
                    if there(t):
                        for c in range(1, CC):
                            fc2(t, c)
                steps(pe, step)

            @block.scalar
            def _(act):
                def step(t, odd):
                    new = t + 1
                    if there(t):
                        act.wait_ge(b1_in, 16)
                        for m in range(G2):
                            wait_e(act, fc1_done, G2, t, m + 1)
                            wait_e(act, hid_lo, G2, t - 1, m + 1)
                            nc.scalar.activation(hid[:, m, :], fc1_bank[m % 2][:, :], ACT.Gelu_apprx_tanh,
                                                 bias=b1[:, bass.ds(t * G2 + m, 1)]).then_inc(gelu_done, 1)
                            wait_e(act, gelu_done, G2, t, m + 1)
                            wait_e(act, fc2_done, CC, t - 1, CC)
                            nc.scalar.activation(hid_h[:, m, :], hid[:, m, :], ACT.Copy).then_inc(hid_hi, 1)
                    if there(new):
                        if not first(new):
                            wait_e(act, w1_in, 16, new, 16)
                            wait_e(act, fc1_done, G2, t, G2)
                            high_part(w1, w1_h).then_inc(w1_hi, 1)
                        wait_e(act, tr_done, 1, new, 1)
                        wait_e(act, g_split, 1, new - 1, 1)
                        for k in range(KT):
                            last = nc.scalar.activation(gT[:, k, :], tr_banks[k][:, :], ACT.Identity,
                                                        bias=cols[:, MLP_B + k:MLP_B + k + 1], scale=cols[:, MLP_G + k:MLP_G + k + 1])
                        last.then_inc(gT_out, 1)
                steps(act, step)

            @block.gpsimd
            def _(pool):
                holds = Links(pool, held)

                def hold():
                    pool.wait_ge(held, holds.base + holds.n)
                    nc.gpsimd.tensor_tensor(idle[:, 1:2], idle[:, 0:1], idle[:, 0:1], ALU.add).then_inc(held, 1)
                    holds.n += 1

                nc.gpsimd.memset(idle[:, :], 0.0).then_inc(held, 1)
                holds.n = 1

                def step(t, odd):
                    new, later = t + 1, t + 2
                    if there(t) and not first(t):
                        wait_e(pool, w2_hi, 1, t, 1)
                        low_part(w2, w2_h, w2_l).then_inc(w2_lo, 1)
                    if there(new) and not first(new):
                        wait_e(pool, w1_hi, 1, new, 1)
                        low_part(w1, w1_h, w1_l).then_inc(w1_lo, 1)
                    if there(later):
                        wait_e(pool, indexed, 1, later, 1)
                        wait_e(pool, gn_done, 1, later - 1, 1)
                        hold()
                        for c in range(CC):
                            nc.gpsimd.indirect_dma_start(out=gx[:, c, :], out_offset=None, in_=x2_rows,
                                                         in_offset=bass.IndirectOffsetOnAxis(ap=next_index[:, c:c + 1], axis=0)).then_inc(gathered, 16)
                    if there(t):
                        wait_e(pool, scattered, 16 * CC, t - 1, 16 * CC)
                        for c in range(CC):
                            wait_e(pool, y_done, CC, t, c + 1)
                            hold()
                            nc.gpsimd.indirect_dma_start(out=out, out_offset=bass.IndirectOffsetOnAxis(ap=index[odd][:, c:c + 1], axis=0),
                                                         in_=yw[:, c, :], in_offset=None, compute_op=ALU.add).then_inc(scattered, 16)
                steps(pool, step, holds, 2 * (CC + 1))
                pool.wait_ge(scattered, 16 * CC * E)

            @block.vector
            def _(dve):
                link = Links(dve, links)
                vec = nc.vector

                def weigh(t, c, odd):
                    wait_e(dve, fc2_done, CC, t, c + 2 if c % 2 == 0 else c + 1)
                    if c == 0:
                        dve.wait_ge(b2_in, 16)
                        wait_e(dve, scattered, 16 * CC, t - 1, 16 * CC)
                    link(vec.tensor_tensor(y[:, c:c + 1, :], fc2_bank[c // 2][:, c % 2 * D:(c % 2 + 1) * D].unsqueeze(1), b2[:, bass.ds(t, 1), :], ALU.add))
                    vec.tensor_scalar(yw[:, c, :], y[:, c, :], share[odd][:, c:c + 1], None, ALU.mult).then_inc(y_done, 1)

                def normalise(e, part):
                    if part == 0:
                        wait_e(dve, gathered, 16 * CC, e, 16 * CC)
                    if part < 2:
                        for c in (2 * part, 2 * part + 1):
                            ins = vec.bn_stats(stats[:, c, :], gx[:, c, :])
                        link(ins)
                    elif part == 2:
                        moments(nc, link, stats, mean[:, :], var[:, :], vt[:, :])
                    elif part < 6:
                        for k in range((part - 3) * 4, min(RSQRT_OPS, (part - 2) * 4)):
                            link(rsqrt_op(nc, k, var[:, :], rstd[:, :], vt[:, :]))
                    elif part == 6:
                        wait_e(dve, tr_done, 1, e - 1, 1)
                        for c in range(CC):
                            last = vec.tensor_scalar(gn[:, c, :], gx[:, c, :], mean[:, c:c + 1], rstd[:, c:c + 1], ALU.subtract, ALU.mult)
                        last.then_inc(gn_done, 1)

                def step(t, odd):
                    new, later, latest = t + 1, t + 2, t + 3
                    if there(t) and not first(t):
                        wait_e(dve, w2_in, 16, t, 16)
                        wait_e(dve, fc2_done, CC, t - 1, CC)
                        vec.tensor_copy(w2_h[:, :, :], w2[:, :, :]).then_inc(w2_hi, 1)
                    for m in range(G2):
                        if there(t):
                            wait_e(dve, hid_hi, G2, t, m + 1)
                            wait_e(dve, fc2_done, CC, t - 1, CC)
                            vec.tensor_tensor(hid_l[:, m, :], hid[:, m, :], hid_h[:, m, :].bitcast(F32), ALU.subtract).then_inc(hid_lo, 1)
                        if there(new) and m < 6:
                            normalise(new, m)
                    if there(later):
                        wait_e(dve, rec_done, 1, later, 1)
                        wait_e(dve, spread_done, 1, later - 1, 1)
                        vec.tensor_copy(rec32[:, :], rec_bank[0:32, 0:48]).then_inc(rec_out, 1)
                    if there(new):
                        normalise(new, 6)
                        wait_e(dve, indexed, 1, new, 1)
                        wait_e(dve, y_done, CC, new - 2, CC)
                        wait_e(dve, scattered, 16 * CC, new - 2, 16 * CC)
                        link(vec.tensor_copy(share[1 - odd][:, :], next_share[:, :]))
                        link(vec.tensor_copy(index[1 - odd][:, :], next_index[:, :]))
                    if there(later):
                        wait_e(dve, spread_done, 1, later, 1)
                        wait_e(dve, gathered, 16 * CC, later - 1, 16 * CC)
                        link(vec.tensor_tensor(picked[:, :, :], rec_bank[:, 64:112].rearrange("p (n q) -> p n q", q=4),
                                               quarter[:, :].unsqueeze(1).to_broadcast([P, 3 * CC, 4]), ALU.mult))
                        link(vec.tensor_reduce(fields[:, :, :].rearrange("p f c -> p (f c)"), picked[:, :, :], AX, ALU.add))
                        link(vec.tensor_tensor(next_share[:, :], fields[:, 1, :], fields[:, 2, :], ALU.add))
                        vec.tensor_copy(next_index[:, :], fields[:, 0, :]).then_inc(indexed, 1)
                    if there(new):
                        wait_e(dve, gT_out, 1, new, 1)
                        wait_e(dve, fc1_done, G2, t, G2)
                        link(vec.tensor_copy(g_h[:, :, :], gT[:, :, :]))
                        vec.tensor_tensor(g_l[:, :, :], gT[:, :, :], g_h[:, :, :].bitcast(F32), ALU.subtract).then_inc(g_split, 1)
                    if there(t):
                        weigh(t, 0, odd)
                        weigh(t, 1, odd)
                    if there(latest):
                        wait_e(dve, rec_done, 1, latest - 1, 1)
                        one = lambda x, n: x[:, :, bass.ds(latest, 1)].to_broadcast([P, TILES, n])
                        vec.tensor_tensor(in_row[:, :, :], one(low, 32), steps32[:, :].unsqueeze(1).to_broadcast([P, TILES, 32]), ALU.is_equal)
                        link(vec.tensor_tensor(in_col[:, :, :], one(high, 16), steps16[:, :].unsqueeze(1).to_broadcast([P, TILES, 16]), ALU.is_equal))
                        vec.tensor_tensor(record[:, :, 0, :], in_col[:, :, :], token[:, :].unsqueeze(2).to_broadcast([P, TILES, 16]), ALU.mult)
                        vec.tensor_tensor(record[:, :, 1, :], in_col[:, :, :], one(gate_hf, 16), ALU.mult)
                        vec.tensor_tensor(record[:, :, 2, :], in_col[:, :, :], one(gate_lf, 16), ALU.mult).then_inc(built, 1)
                    if there(t):
                        weigh(t, 2, odd)
                        weigh(t, 3, odd)
                gate_hf, gate_lf = gate_h[:, :, :].bitcast(F32), gate_l[:, :, :].bitcast(F32)
                steps(dve, step, link, LINKS_EXPERTS)


LINKS_EXPERTS = 54


def tables():
    r = np.arange(P)
    t = [r[:, None] < r[None, :], r[:, None] % E == r[None, :] % E, r[:, None] == r[None, :] % 32, r[:, None] < 0 * r[None, :]]
    return np.concatenate(t, 1).astype(np.float32)


def counts():
    r = np.arange(P)[:, None]
    t = [np.broadcast_to(np.arange(32), (P, 32)), r // 32 == np.arange(4)[None, :], r + P * np.arange(TILES)[None, :]]
    return np.concatenate(t, 1).astype(np.float32)


def laid_out(v):
    f = lambda n: np.asarray(v[n])
    c = np.ascontiguousarray
    pos = (np.arange(T) / max(1, T - 1)).astype(np.float32)
    ang = np.float32(2.0 * np.pi) * pos[:, None] * np.arange(1, 9, dtype=np.float32)[None, :]
    harm = np.stack([np.sin(ang), np.cos(ang)], -1).reshape(T, 16).astype(np.float32)
    halves = lambda n: [f(n)[k * P:(k + 1) * P] for k in range(f(n).shape[0] // P)]
    twice = lambda n: [np.concatenate([f(n), f(n)])]
    cols = np.stack(halves("L0_cond_norm_in_w") + halves("L0_cond_norm_out_w") + halves("L1_cond_ln1_g")
                    + halves("L1_cond_ln1_b") + halves("L1_cond_b_ada") + halves("L1_cond_mlp_g") + halves("L1_cond_mlp_b")
                    + twice("L1_cond_qn_g") + twice("L1_cond_qn_b") + twice("L1_cond_kn_g") + twice("L1_cond_kn_b")
                    + halves("L0_cond_ffn_b1"), 1)
    cols = np.concatenate([cols, np.zeros((P, 30 - cols.shape[1]), cols.dtype)], 1)
    x = f("x")
    return {
        "x": c(x.reshape(TOKENS, D)), "xT": c(x.transpose(0, 2, 1).reshape(NB * D, T)),
        "cond": c(f("cond_1024").T), "cfg": c(f("condB_cfgscale").reshape(NB, 1)), "cols": c(cols),
        "ident": np.eye(P, dtype=np.float32), "harm": c(harm.T),
        "pre_w": c(f("L0_cond_pre_w").T), "harm_w": c(f("L0_cond_harm_w").T), "harm_b": c(f("L0_cond_harm_b")),
        "style_w": c(f("L0_cond_style_w").T), "merge_w": c(f("L0_cond_merge_w").T), "merge_b": c(f("L0_cond_merge_b")),
        "ffn_w1": c(f("L0_cond_ffn_w1").T), "ffn_w2": c(f("L0_cond_ffn_w2").T), "ffn_b2": c(f("L0_cond_ffn_b2")),
        "W_ada": c(f("L1_cond_W_ada").T),
        "wqk": c(f("L1_cond_Wqkv")[:2 * HW]), "wv": c(f("L1_cond_Wqkv")[2 * HW:].T), "wout": c(f("L1_cond_Wout").T),
        "wgate": c(f("L1_cond_Wgate").T),
        "tables": tables(), "counts": counts(), "b1s": c(f("L1_cond_b1s").reshape(E * G2, P).T), "b2s": c(f("L1_cond_b2s")),
        "fc1s": c(f("L1_cond_fc1s").transpose(0, 2, 1).reshape(E * D, DD)),
        "fc2s": c(f("L1_cond_fc2s").transpose(0, 2, 1).reshape(E * DD, D)),
        "center": np.kron(np.eye(2), np.eye(HD) - np.ones((HD, HD)) / HD).astype(np.float32),
    }


_ORDER = ["x", "xT", "cond", "cfg", "cols", "ident", "harm", "pre_w", "harm_w", "harm_b", "style_w", "merge_w", "merge_b",
          "ffn_w1", "ffn_w2", "ffn_b2", "W_ada", "wqk", "wv", "wout", "wgate", "center", "tables", "counts", "b1s", "b2s",
          "fc1s", "fc2s"]


def kernel(**inputs):
    import concourse.bacc as bacc
    from concourse.bass_utils import run_bass_kernel_spmd

    nc = bacc.Bacc("TRN2", target_bir_lowering=False, num_devices=1)
    laid = laid_out(inputs)
    arrays, args = {}, {}
    for name in _ORDER:
        arrays["in_" + name] = laid[name]
        args[name] = nc.dram_tensor("in_" + name, laid[name].shape, mybir.dt.from_np(laid[name].dtype), kind="ExternalInput").ap()
    out = nc.dram_tensor("out", (TOKENS, D), F32, kind="ExternalOutput").ap()
    build(nc, args, out)
    result = run_bass_kernel_spmd(nc, [arrays], core_ids=[0])
    return result.results[0]["out"].reshape(NB, T, D)
```
